# Optimizing a Trainium2 kernel written in Bass

```python
import numpy as np
import jax
import jax.numpy as jnp

def _softmax(x, axis=-1):
    return jax.nn.softmax(x, axis=axis)

def _gelu(x):
    return jax.nn.gelu(x, approximate=True)

def _silu(x):
    return jax.nn.silu(x)

def _sigmoid(x):
    return jax.nn.sigmoid(x)

def _layernorm(x, axis=-1, eps=1e-05):
    m = jnp.mean(x, axis=axis, keepdims=True)
    v = jnp.var(x, axis=axis, keepdims=True)
    return (x - m) / jnp.sqrt(v + eps)

def _scatter_add(tgt, idx, src, axis=0):
    return tgt.at[idx].add(src)

def _segment_sum(src, seg, n):
    return jax.ops.segment_sum(src, seg, n)
kernel_name = 'mk_xattn_ffn_d1_seqx_r8_9eff33'

def setup_inputs(seed: int=0):
    np.random.seed(seed)
    _w = jnp.asarray

    def _rec_inputs():
        import jax
        import jax.numpy as jnp
        _rk = jax.random.key(seed)
        x = 0.01048 + 0.1018 * jax.random.normal(jax.random.fold_in(_rk, 1), (4, 256, 256), jnp.float32)
        _lenS = 256 - jax.random.randint(jax.random.fold_in(_rk, 7), (4,), 0, max(1, 256 // 4) + 1, jnp.int32)
        _lenS2 = 256 - jax.random.randint(jax.random.fold_in(_rk, 8), (4,), 0, max(1, 256 // 4) + 1, jnp.int32)
        _ctx_512P = jax.random.normal(jax.random.fold_in(_rk, 11), (4, 16, 64), jnp.float32)
        _ctx_512c = jax.random.dirichlet(jax.random.fold_in(_rk, 511), 0.3 * jnp.ones((16,), jnp.float32), (4, 256))
        _ctx_512t = jnp.einsum('bsk,bkd->bsd', _ctx_512c, _ctx_512P)
        _ctx_512t = _ctx_512t * jax.lax.rsqrt(jnp.mean(jnp.square(_ctx_512t)) + 1e-12) * 0.953939
        ctx_512 = -0.000292821 + 1.00034 * (_ctx_512t + 0.3 * jax.random.normal(jax.random.fold_in(_rk, 611), (4, 256, 64), jnp.float32))
        return (x, ctx_512)
    x, ctx_512 = _rec_inputs()

    def _L0_xattn_setup():
        import jax, jax.numpy as jnp
        import numpy as np
        LRELU_ALPHA = 0.2
        MASK_VAL = -10000000000.0
        B, N, F_IN = (4, 256, 64)
        H, F_OUT = (8, 32)
        F_HID = H * F_OUT

        def gat_layer(x, adj, W, a_self, a_neigh, b):
            feat = jnp.einsum('nf,hfo->hno', x, W)
            attn_self = jnp.einsum('hno,ho->hn', feat, a_self)
            attn_neigh = jnp.einsum('hno,ho->hn', feat, a_neigh)
            e = attn_self[:, :, None] + attn_neigh[:, None, :]
            e = jax.nn.leaky_relu(e, LRELU_ALPHA)
            e = e + MASK_VAL * (1.0 - adj)[None, :, :]
            alpha = jax.nn.softmax(e, axis=-1)
            out = jnp.einsum('hnm,hmo->hno', alpha, feat) + b[:, None, :]
            out = jnp.transpose(out, (1, 0, 2)).reshape(out.shape[1], -1)
            return jax.nn.elu(out)
        key = jax.random.key(seed)
        ks = jax.random.split(key, 10)
        feats = jax.random.normal(ks[0], (B, N, F_IN), dtype=jnp.float32)
        a = (jax.random.uniform(ks[1], (B, N, N)) < 0.01).astype(jnp.float32)
        adj = jnp.maximum(a, jnp.eye(N, dtype=jnp.float32)[None])
        s0 = 1.0 / np.sqrt(F_IN)
        s1 = 1.0 / np.sqrt(F_HID)
        return {'feats': feats, 'adj': adj, 'W0': jax.random.normal(ks[2], (H, F_IN, F_OUT), dtype=jnp.float32) * s0, 'a_self0': jax.random.normal(ks[3], (H, F_OUT), dtype=jnp.float32) * 0.1, 'a_neigh0': jax.random.normal(ks[4], (H, F_OUT), dtype=jnp.float32) * 0.1, 'b0': jnp.zeros((H, F_OUT), dtype=jnp.float32), 'W1': jax.random.normal(ks[5], (H, F_HID, F_OUT), dtype=jnp.float32) * s1, 'a_self1': jax.random.normal(ks[6], (H, F_OUT), dtype=jnp.float32) * 0.1, 'a_neigh1': jax.random.normal(ks[7], (H, F_OUT), dtype=jnp.float32) * 0.1, 'b1': jnp.zeros((H, F_OUT), dtype=jnp.float32)}
    _L0_xattn_all = _L0_xattn_setup()
    _L0_xattn_in = {k: v for k, v in _L0_xattn_all.items() if k in ('W0', 'a_self0', 'a_neigh0', 'b0', 'W1', 'a_self1', 'a_neigh1', 'b1')}
    del _L0_xattn_all

    def _L0_ffn_setup():
        import jax, jax.numpy as jnp
        import numpy as np
        ROPE_THETA = 1000000.0
        TOP_K = 2

        def rmsnorm(x, w, eps=1e-06):
            xf = x.astype(jnp.float32)
            n = jax.lax.rsqrt(jnp.mean(xf * xf, axis=-1, keepdims=True) + eps)
            return (xf * n).astype(x.dtype) * w

        def rope_tables(seq_len, head_dim):
            freqs = 1.0 / ROPE_THETA ** (jnp.arange(0, head_dim, 2, dtype=jnp.float32) / head_dim)
            t = jnp.arange(seq_len, dtype=jnp.float32)
            f = jnp.outer(t, freqs)
            return (jnp.cos(f), jnp.sin(f))

        def apply_rope(x, cos, sin):
            half = x.shape[-1] // 2
            x1, x2 = (x[..., :half], x[..., half:])
            c = cos[None, None]
            s = sin[None, None]
            return jnp.concatenate([x1 * c - x2 * s, x2 * c + x1 * s], axis=-1)
        key = jax.random.key(seed)
        ks = jax.random.split(key, 8)
        B, S, D = (2, 256, 256)
        Hq, Hkv, hd = (16, 4, 128)
        E, I = (8, 176)
        sc = 0.02
        return {'hidden': jax.random.normal(ks[0], (B, S, D), jnp.float32), 'attn_norm_w': jnp.ones((D,), jnp.float32), 'q_w': jax.random.normal(ks[1], (Hq * hd, D), jnp.float32) * sc, 'k_w': jax.random.normal(ks[2], (Hkv * hd, D), jnp.float32) * sc, 'v_w': jax.random.normal(ks[3], (Hkv * hd, D), jnp.float32) * sc, 'o_w': jax.random.normal(ks[4], (D, Hq * hd), jnp.float32) * sc, 'q_norm_w': jnp.ones((hd,), jnp.float32), 'k_norm_w': jnp.ones((hd,), jnp.float32), 'ffn_norm_w': jnp.ones((D,), jnp.float32), 'gate_w': jax.random.normal(ks[5], (E, D), jnp.float32) * sc, 'wg': jax.random.normal(ks[6], (E, I, D), jnp.float32) * sc, 'wu': jax.random.normal(ks[7], (E, I, D), jnp.float32) * sc, 'wd': jax.random.normal(jax.random.fold_in(key, 99), (E, D, I), jnp.float32) * sc}
    _L0_ffn_all = _L0_ffn_setup()
    _L0_ffn_in = {k: v for k, v in _L0_ffn_all.items() if k in ('attn_norm_w', 'q_w', 'k_w', 'v_w', 'o_w', 'q_norm_w', 'k_norm_w', 'ffn_norm_w', 'gate_w', 'wg', 'wu', 'wd')}
    del _L0_ffn_all
    return {'x': x, 'ctx_512': ctx_512, 'L0_xattn_W0': _L0_xattn_in['W0'], 'L0_xattn_a_self0': _L0_xattn_in['a_self0'], 'L0_xattn_a_neigh0': _L0_xattn_in['a_neigh0'], 'L0_xattn_b0': _L0_xattn_in['b0'], 'L0_xattn_W1': _L0_xattn_in['W1'], 'L0_xattn_a_self1': _L0_xattn_in['a_self1'], 'L0_xattn_a_neigh1': _L0_xattn_in['a_neigh1'], 'L0_xattn_b1': _L0_xattn_in['b1'], 'L0_ffn_attn_norm_w': _L0_ffn_in['attn_norm_w'], 'L0_ffn_q_w': _L0_ffn_in['q_w'], 'L0_ffn_k_w': _L0_ffn_in['k_w'], 'L0_ffn_v_w': _L0_ffn_in['v_w'], 'L0_ffn_o_w': _L0_ffn_in['o_w'], 'L0_ffn_q_norm_w': _L0_ffn_in['q_norm_w'], 'L0_ffn_k_norm_w': _L0_ffn_in['k_norm_w'], 'L0_ffn_ffn_norm_w': _L0_ffn_in['ffn_norm_w'], 'L0_ffn_gate_w': _L0_ffn_in['gate_w'], 'L0_ffn_wg': _L0_ffn_in['wg'], 'L0_ffn_wu': _L0_ffn_in['wu'], 'L0_ffn_wd': _L0_ffn_in['wd']}

def reference(x, ctx_512, L0_xattn_W0, L0_xattn_a_self0, L0_xattn_a_neigh0, L0_xattn_b0, L0_xattn_W1, L0_xattn_a_self1, L0_xattn_a_neigh1, L0_xattn_b1, L0_ffn_attn_norm_w, L0_ffn_q_w, L0_ffn_k_w, L0_ffn_v_w, L0_ffn_o_w, L0_ffn_q_norm_w, L0_ffn_k_norm_w, L0_ffn_ffn_norm_w, L0_ffn_gate_w, L0_ffn_wg, L0_ffn_wu, L0_ffn_wd):
    import jax
    import jax.numpy as jnp

    def _L0_xattn_ref(feats, adj, W0, a_self0, a_neigh0, b0, W1, a_self1, a_neigh1, b1):
        import jax, jax.numpy as jnp
        import numpy as np
        LRELU_ALPHA = 0.2
        MASK_VAL = -10000000000.0
        B, N, F_IN = (4, 256, 64)
        H, F_OUT = (8, 32)
        F_HID = H * F_OUT

        def gat_layer(x, adj, W, a_self, a_neigh, b):
            feat = jnp.einsum('nf,hfo->hno', x, W)
            attn_self = jnp.einsum('hno,ho->hn', feat, a_self)
            attn_neigh = jnp.einsum('hno,ho->hn', feat, a_neigh)
            e = attn_self[:, :, None] + attn_neigh[:, None, :]
            e = jax.nn.leaky_relu(e, LRELU_ALPHA)
            e = e + MASK_VAL * (1.0 - adj)[None, :, :]
            alpha = jax.nn.softmax(e, axis=-1)
            out = jnp.einsum('hnm,hmo->hno', alpha, feat) + b[:, None, :]
            out = jnp.transpose(out, (1, 0, 2)).reshape(out.shape[1], -1)
            return jax.nn.elu(out)

        def per_graph(x, a):
            h = gat_layer(x, a, W0, a_self0, a_neigh0, b0)
            return gat_layer(h, a, W1, a_self1, a_neigh1, b1)
        return jax.vmap(per_graph)(feats, adj)

    def _L0_ffn_ref(hidden, attn_norm_w, q_w, k_w, v_w, o_w, q_norm_w, k_norm_w, ffn_norm_w, gate_w, wg, wu, wd):
        import jax, jax.numpy as jnp
        import numpy as np
        ROPE_THETA = 1000000.0
        TOP_K = 2

        def rmsnorm(x, w, eps=1e-06):
            xf = x.astype(jnp.float32)
            n = jax.lax.rsqrt(jnp.mean(xf * xf, axis=-1, keepdims=True) + eps)
            return (xf * n).astype(x.dtype) * w

        def rope_tables(seq_len, head_dim):
            freqs = 1.0 / ROPE_THETA ** (jnp.arange(0, head_dim, 2, dtype=jnp.float32) / head_dim)
            t = jnp.arange(seq_len, dtype=jnp.float32)
            f = jnp.outer(t, freqs)
            return (jnp.cos(f), jnp.sin(f))

        def apply_rope(x, cos, sin):
            half = x.shape[-1] // 2
            x1, x2 = (x[..., :half], x[..., half:])
            c = cos[None, None]
            s = sin[None, None]
            return jnp.concatenate([x1 * c - x2 * s, x2 * c + x1 * s], axis=-1)
        B, S, D = hidden.shape
        hd = q_norm_w.shape[0]
        Hq = q_w.shape[0] // hd
        Hkv = k_w.shape[0] // hd
        n_rep = Hq // Hkv
        h = rmsnorm(hidden, attn_norm_w)
        q = (h @ q_w.T).reshape(B, S, Hq, hd)
        k = (h @ k_w.T).reshape(B, S, Hkv, hd)
        v = (h @ v_w.T).reshape(B, S, Hkv, hd)
        q = rmsnorm(q, q_norm_w).transpose(0, 2, 1, 3)
        k = rmsnorm(k, k_norm_w).transpose(0, 2, 1, 3)
        v = v.transpose(0, 2, 1, 3)
        cos, sin = rope_tables(S, hd)
        q = apply_rope(q, cos, sin)
        k = apply_rope(k, cos, sin)
        k = jnp.repeat(k, n_rep, axis=1)
        v = jnp.repeat(v, n_rep, axis=1)
        scale = 1.0 / jnp.sqrt(jnp.float32(hd))
        scores = jnp.einsum('bhqd,bhkd->bhqk', q, k) * scale
        causal = jnp.tril(jnp.ones((S, S), bool))
        scores = jnp.where(causal[None, None], scores, jnp.finfo(scores.dtype).min)
        attn = jnp.einsum('bhqk,bhkd->bhqd', jax.nn.softmax(scores, axis=-1), v)
        attn = attn.transpose(0, 2, 1, 3).reshape(B, S, Hq * hd)
        hidden = hidden + attn @ o_w.T
        h2 = rmsnorm(hidden, ffn_norm_w)
        T = B * S
        E = gate_w.shape[0]
        tok = h2.reshape(T, D)
        probs = jax.nn.softmax(tok @ gate_w.T, axis=-1)
        topv, topi = jax.lax.top_k(probs, TOP_K)
        topw = topv / (jnp.sum(topv, axis=-1, keepdims=True) + 1e-09)
        combine = jnp.zeros((T, E), tok.dtype).at[jnp.arange(T)[:, None], topi].set(topw)
        eg = jnp.einsum('td,eid->eti', tok, wg)
        eu = jnp.einsum('td,eid->eti', tok, wu)
        eo = jnp.einsum('eti,edi->etd', jax.nn.silu(eg) * eu, wd)
        moe_out = jnp.einsum('te,etd->td', combine, eo).reshape(B, S, D)
        return hidden + moe_out
    x = x + _L0_xattn_ref(ctx_512, _layernorm(x, axis=-1), L0_xattn_W0, L0_xattn_a_self0, L0_xattn_a_neigh0, L0_xattn_b0, L0_xattn_W1, L0_xattn_a_self1, L0_xattn_a_neigh1, L0_xattn_b1)
    x = x + _L0_ffn_ref(_layernorm(x, axis=-1), L0_ffn_attn_norm_w, L0_ffn_q_w, L0_ffn_k_w, L0_ffn_v_w, L0_ffn_o_w, L0_ffn_q_norm_w, L0_ffn_k_norm_w, L0_ffn_ffn_norm_w, L0_ffn_gate_w, L0_ffn_wg, L0_ffn_wu, L0_ffn_wd)
    return x

_drawn_inputs = setup_inputs


def setup_inputs(seed=0):
    import zlib

    import numpy as np

    out = dict(_drawn_inputs(seed))
    spreads = {'L0_xattn_b0': (0.0, 0.1),
     'L0_xattn_b1': (0.0, 0.1),
     'L0_ffn_attn_norm_w': (1.0, 0.6),
     'L0_ffn_q_norm_w': (1.0, 0.6),
     'L0_ffn_k_norm_w': (1.0, 0.6),
     'L0_ffn_ffn_norm_w': (1.0, 0.6)}
    factors = {'L0_ffn_gate_w': 8.0, 'L0_ffn_wg': 8.0, 'L0_ffn_wu': 8.0, 'L0_ffn_wd': 8.0}
    for name, (base, spread) in spreads.items():
        noise = np.random.default_rng([zlib.crc32(name.encode()), seed]).standard_normal(out[name].shape)
        drawn = base * np.exp(spread * noise) if base else spread * noise
        out[name] = jnp.asarray(drawn.astype(out[name].dtype))
    for name, factor in factors.items():
        out[name] = (out[name] * factor).astype(out[name].dtype)
    return out
```

```python
import concourse.bass as bass
from concourse import mybir
from contextlib import ExitStack
import numpy as np

F32 = mybir.dt.float32
I32 = mybir.dt.int32
BF16 = mybir.dt.bfloat16
ALU = mybir.AluOpType
ACT = mybir.ActivationFunctionType
AX = mybir.AxisListType

P = 128
B, N, D = 4, 256, 256
T = N // P
KT = D // P
F_IN = 64
H, FO = 8, 32
FE = FO + 1
NP = 3
KZ = NP * 2 * H
HQ, HKV, HD = 16, 4, 128
G = HQ // HKV
E, I = 8, 176
EI = E * I
JT = EI // P
NU = 2 * T * 2
QU = (HQ + HKV) // G * T
LN_EPS, RMS_EPS = 1e-5, 1e-6
SCALE = float(HD) ** -0.5
MASKED = -1e30
MAGIC = 0x5F3759DF

C_ID = 0
C_CAUSAL = C_ID + P
C_COS = C_CAUSAL + P
C_SIN = C_COS + T * HD
C_PICK = C_SIN + T * HD
C_ONE = C_PICK + H
C_SELF = C_ONE + H
C_NEIGH = C_SELF + 1
C_TRI = C_NEIGH + 1
C_END = C_TRI + E * E


def constants():
    c = np.zeros((P, C_END), np.float32)
    c[:, C_ID:C_ID + P] = np.eye(P)
    c[:, C_CAUSAL:C_CAUSAL + P] = np.where(np.arange(P)[None, :] > np.arange(P)[:, None], MASKED, 0.0)
    freqs = (np.float32(1.0) / np.float32(1e6) ** (np.arange(0, HD, 2, dtype=np.float32) / np.float32(HD))).astype(np.float32)
    angle = np.outer(np.arange(N, dtype=np.float32), freqs).astype(np.float32)
    cos, sin = np.cos(angle), np.sin(angle)
    for t in range(T):
        rows = slice(t * P, (t + 1) * P)
        c[:, C_COS + t * HD:C_COS + (t + 1) * HD] = np.concatenate([cos[rows], cos[rows]], 1)
        c[:, C_SIN + t * HD:C_SIN + (t + 1) * HD] = np.concatenate([-sin[rows], sin[rows]], 1)
    for p in range(NP):
        for h in range(H):
            self_row, neigh_row = p * 2 * H + h, p * 2 * H + H + h
            c[neigh_row, C_PICK + h] = 1.0
            c[self_row, C_ONE + h] = 1.0
            c[self_row, C_SELF] = 1.0
            c[neigh_row, C_NEIGH] = 1.0
    for e in range(E):
        c[:, C_TRI + e * E:C_TRI + e * E + e] = 1.0
    spread = np.tile(np.repeat(np.eye(E, dtype=np.float32), I, axis=1), (NP, 1))
    return c, spread


N_A, N_B = 81, 143


STEPS = 41


def work(s):
    w = []
    if s < 12:
        w.append(("qkv", s))
    u = s - 3
    if u in (0, 1):
        w.append(("turn", u))
    if 4 <= u < 12:
        w.append(("turn", u - 2))
    if 9 <= s < 9 + 2 * HKV:
        g, t = divmod(s - 9, 2)
        w += [("score", 3 * g)] if t == 0 else [("score", 3 * g + 1), ("score", 3 * g + 2)]
    if 13 <= s < 13 + 2 * HKV:
        g, t = divmod(s - 13, 2)
        w += [("probT", 3 * g)] if t == 0 else [("probT", 3 * g + 1), ("probT", 3 * g + 2)]
    if 14 <= s < 14 + 2 * HKV:
        w.append(("av", s - 14))
    if s in (22, 23):
        w.append(("oproj", s - 22))
    if s in (25, 26):
        w.append(("h2T", s - 25))
    if s == 27:
        w.append(("gate", 0))
    if 27 <= s < 27 + JT:
        w.append(("updown", s - 27))
    if s == 29:
        w += [("mixT", 0), ("mixT", 1)]
    if s in (31, 32, 33, 35, 37, 38):
        w.append(("mix", (31, 32, 33, 35, 37, 38).index(s)))
    if s in (39, 40):
        w.append(("down", s - 39))
    return w


def summed(s):
    return [n for kind, n in work(s - 2) if kind == "score"]


BANKS = 4
ORDER = [w for s in range(STEPS) for w in work(s)]
FILLS = len(ORDER) // BANKS
assert len(ORDER) == BANKS * FILLS
PLACE = {w: divmod(n, BANKS)[::-1] for n, w in enumerate(ORDER)}


def block_program(nc, x, ctxT, w0, w1, gat_rows, norm_cols, qk_rows, wqkv, wo, wgate, wgu, wd, consts, spread, out):
    ctx = ExitStack()
    with ctx:
        def sb(name, shape, dt=F32):
            return ctx.enter_context(nc.sbuf_tensor(name, shape, dt))

        def pb(name, shape, dt=F32):
            return ctx.enter_context(nc.psum_tensor(name, shape, dt))

        def sem(name):
            return ctx.enter_context(nc.semaphore(name))

        cst = sb("cst", [P, C_END])
        ident = cst[:, C_ID:C_ID + P]
        identb = sb("identb", [P, P], BF16)
        causal = sb("causal", [P, P], BF16)
        expert_rows = sb("expert_rows", [NP * E, EI], BF16)
        rows = sb("rows", [P, 6 * D])
        w0x = sb("w0x", [F_IN, D + 2 * H])
        w1x = sb("w1x", [P, KT, D + 2 * H])
        cols = sb("cols", [P, 2 * KT])
        qkw = sb("qkw", [P, 2 * HD])
        rope_c = sb("rope_c", [P, 2, T, HD])
        rope_s = sb("rope_s", [P, 2, T, HD])
        wqkv_sb = sb("wqkv_sb", [P, KT, (HQ + 2 * HKV) * HD])
        wo_sb = sb("wo_sb", [P, HQ, D])
        wgate_sb = sb("wgate_sb", [P, KT, E])
        wgu_sb = sb("wgu_sb", [P, 2, KT, EI])
        wd_sb = sb("wd_sb", [P, JT, D])
        xin = sb("xin", [P, T, D])
        cin = sb("cin", [F_IN, N])
        stats = sb("stats", [P, T, 6])
        mv = sb("mv", [P, T, 2])
        rs_v = sb("rs_v", [P, 2 * T])
        rs_y = sb("rs_y", [P, 2 * T])
        rs_a = sb("rs_a", [P, 2 * T])
        maskv = sb("maskv", [P, T, N])
        feat = sb("feat", [P, T, H, FE])
        sn_res = sb("sn_res", [P, T, 2 * H])
        parts = sb("parts", [P, T, NP, 2 * H], BF16)
        partsT = sb("partsT", [KZ, N], BF16)
        pair_l = sb("pair_l", [KZ, N], BF16)
        pair_r = sb("pair_r", [KZ, H, N], BF16)
        zs = sb("zs", [P, 2, 2 * N])
        lr = sb("lr", [P, 2 * N])
        tt = sb("tt", [P, 2, 2, N])
        gmx = sb("gmx", [P, 2, 2])
        gneg = sb("gneg", [P, 2, 2])
        gpT = sb("gpT", [P, 2, 2, T, P])
        gsum = sb("gsum", [P, H])
        go = sb("go", [P, T, D])
        wprod = go[:, 0, :]
        gex = sb("gex", [P, T, D])
        gres = sb("gres", [P, T, D])
        gT = sb("gT", [P, KT, N])
        x1 = sb("x1", [P, T, D])
        hid = sb("hid", [P, T, D])
        hn = gres
        hT = sb("hT", [P, KT, N])
        early = sb("early", [P, 6, G * HD])[:, :, :]
        raw, sq = early[:, 0:3, :], early[:, 3:6, :]
        v_sb = sb("v_sb", [P, T, HKV * HD])
        m1 = sb("m1", [P, G * HD])
        m2 = sb("m2", [P, 2, G * HD])
        rot = sb("rot", [P, 4, G * HD])
        ssq = sb("ssq", [P, QU, G])
        qk_v = sb("qk_v", [P, 2 * G])
        qk_y = sb("qk_y", [P, 2 * G])
        qk_a = sb("qk_a", [P, 2 * G])
        rk = sb("rk", [P, T, G])
        rq = sb("rq", [P, HKV, T, G])
        qT = sb("qT", [P, HQ, N])
        kT = sb("kT", [P, HKV, N])
        smx = sb("smx", [P, 3 * HKV, G])
        sneg = sb("sneg", [P, 3 * HKV, G])
        ssum = sb("ssum", [P, 3 * HKV, G])
        srcp = sb("srcp", [P, 3 * HKV, G])
        prob = sb("prob", [P, 6, 2 * N])
        pT0 = sb("pT0", [P, G, P])
        pT1 = sb("pT1", [P, T, G, P])
        oT = qT
        late = rot[:, :, :].rearrange("p a (t d) -> p a t d", t=T)
        hid2, osum, h2n = late[:, 0], late[:, 1], late[:, 2]
        ss2 = sb("ss2", [P, T])
        tokT = late[:, 3]
        lg = sb("lg", [P, T, E])
        lmx = sb("lmx", [P, T])
        lex = sb("lex", [P, T, E])
        cmp1 = m1[:, N:N + T * E * E].rearrange("p (t e j) -> p t e j", t=T, e=E)
        cmp2 = m1[:, N + T * E * E:N + 2 * T * E * E].rearrange("p (t e j) -> p t e j", t=T, e=E)
        rank = sb("rank", [P, T, E])
        mixp = sb("mixp", [P, T, NP, E], BF16)
        mixT = sb("mixT", [NP * E, N], BF16)
        th = pT1[:, :, :, :].rearrange("p m h q -> p (m h q)")[:, 0:3 * N].rearrange("p (a n) -> p a n", a=3)
        ga = m1[:, 0:N]
        ah = early.rearrange("p a c -> p (a c)")[:, 0:JT * N].rearrange("p (j n) -> p j n", j=JT)
        yo = rows[:, 0:T * D].rearrange("p (t d) -> p t d", t=T)
        spread_in = ah[0:NP * E, :, :].rearrange("p j n -> p (j n)")[:, 0:EI]

        zb = [pb(f"zb{k}", [P, 512]) for k in range(2)]
        tb = pb("tb", [P, 512])
        ob = pb("ob", [P, 512])
        bank = [pb(f"bank{k}", [P, 512]) for k in range(BANKS)]

        in_cst, in_gat, in_x, in_c = sem("in_cst"), sem("in_gat"), sem("in_x"), sem("in_c")
        in_qkv, in_o, in_gu, in_d = sem("in_qkv"), sem("in_o"), sem("in_gu"), sem("in_d")
        out_free = sem("out_free")
        x_used, c_used = sem("x_used"), sem("c_used")
        setup_v, setup_done = sem("setup_v"), sem("setup_done")
        dve_a = sem("dve_a")
        z_full = [sem(f"z_full{k}") for k in range(2)]
        z_free = [sem(f"z_free{k}") for k in range(2)]
        t_full, t_free = sem("t_full"), sem("t_free")
        parts_ready, pair_ready = sem("parts_ready"), sem("pair_ready")
        lrelu_done, score_ready, shifted = sem("lrelu_done"), sem("score_ready"), sem("shifted")
        pv_done, o_free = sem("pv_done"), sem("o_free")
        gout_ready, gexp_ready, gres_ready, hn_ready = sem("gout_ready"), sem("gexp_ready"), sem("gres_ready"), sem("hn_ready")
        dve_b = sem("dve_b")
        full = [sem(f"full{k}") for k in range(BANKS)]
        free = [sem(f"free{k}") for k in range(BANKS)]
        raw_ready, m2_ready, rot_ready = sem("raw_ready"), sem("m2_ready"), sem("rot_ready")
        sneg_ready, srcp_ready, prob_ready = sem("sneg_ready"), sem("srcp_ready"), sem("prob_ready")
        hid2_ready, osum_ready, h2n_ready = sem("hid2_ready"), sem("osum_ready"), sem("h2n_ready")
        lneg_ready, lexp_ready, mix_ready, tanh_ready, y_ready = sem("lneg_ready"), sem("lexp_ready"), sem("mix_ready"), sem("tanh_ready"), sem("y_ready")

        block = ctx.enter_context(nc.Block())

        def z_value(b, l, n):
            return b * 10 + l * 5 + n + 1

        def t_value(b, l, n):
            return b * 20 + l * 10 + n + 1

        def filled(eng, b, w):
            k, i = PLACE[w]
            eng.wait_ge(full[k], b * FILLS + i + 1)

        def emptied(eng, b, w):
            k, i = PLACE[w]
            eng.wait_ge(free[k], b * FILLS + i + 2)

        def emptied_all(eng, b, ws):
            last = {}
            for w in ws:
                last[PLACE[w][0]] = w
            for w in last.values():
                emptied(eng, b, w)

        def bank_of(w):
            return bank[PLACE[w][0]]

        def full_of(w):
            return full[PLACE[w][0]]

        def free_of(w):
            return free[PLACE[w][0]]

        @block.sync
        def _(sp):
            sp.dma_start(cst[:, :], consts).then_inc(in_cst, 16)
            sp.dma_start(spread_in, spread).then_inc(in_cst, 16)
            sp.dma_start(cin[:, :], ctxT[0]).then_inc(in_c, 16)
            sp.dma_start(xin[:, :, :], x[0].rearrange("(t p) d -> p t d", p=P)).then_inc(in_x, 16)
            sp.dma_start(w0x[:, 0:D], w0).then_inc(in_gat, 16)
            sp.dma_start(w1x[:, :, 0:D], w1.rearrange("(k p) n -> p k n", p=P)).then_inc(in_gat, 16)
            sp.dma_start(rows[:, :], gat_rows).then_inc(in_gat, 16)
            sp.dma_start(cols[:, :], norm_cols).then_inc(in_gat, 16)
            sp.dma_start(qkw[:, :], qk_rows).then_inc(in_gat, 16)
            sp.dma_start(wqkv_sb[:, :, :], wqkv.rearrange("(k p) n -> p k n", p=P)).then_inc(in_qkv, 16)
            sp.dma_start(wo_sb[:, :, :], wo.rearrange("(h p) n -> p h n", p=P)).then_inc(in_o, 16)
            sp.dma_start(wgate_sb[:, :, :], wgate.rearrange("(k p) n -> p k n", p=P)).then_inc(in_gu, 16)
            for m in range(2):
                sp.dma_start(wgu_sb[:, m, :, :], wgu[m].rearrange("(k p) n -> p k n", p=P)).then_inc(in_gu, 16)
            sp.dma_start(wd_sb[:, :, :], wd.rearrange("(j p) n -> p j n", p=P)).then_inc(in_d, 16)

            def load_inputs(b):
                sp.wait_ge(c_used, b)
                sp.dma_start(cin[:, :], ctxT[bass.ds(b, 1)].squeeze(0) if not isinstance(b, int) else ctxT[b]).then_inc(in_c, 16)
                sp.wait_ge(x_used, b)
                src = x[bass.ds(b, 1)].squeeze(0) if not isinstance(b, int) else x[b]
                sp.dma_start(xin[:, :, :], src.rearrange("(t p) d -> p t d", p=P)).then_inc(in_x, 16)

            def store(b):
                dst = out[bass.ds(b, 1)].squeeze(0) if not isinstance(b, int) else out[b]
                for t in range(T):
                    sp.wait_ge(y_ready, b * T + t + 1)
                    sp.dma_start(dst[t * P:(t + 1) * P, :], yo[:, t, :]).then_inc(out_free, 16)

            load_inputs(1)
            with sp.Fori(0, B - 2) as b:
                load_inputs(b + 2)
                store(b)
            store(B - 2)
            store(B - 1)
            sp.wait_ge(out_free, 16 * T * (B + 1))

        @block.tensor
        def _(pe):
            def gat(b, a):
                if a in (1, 19):
                    l = (a - 1) // 18
                    if l == 0:
                        pe.wait_ge(in_c, (b + 1) * 16)
                    else:
                        pe.wait_ge(t_free, t_value(b, 0, 9) + 1)
                    for t in range(T):
                        pe.wait_ge(z_free[t], z_value(b, l, 0))
                        if l == 0:
                            pe.matmul(zb[t][:, 0:D + 2 * H], cin[:, t * P:(t + 1) * P], w0x[:, :], start=True, stop=True)\
                              .then_inc(z_full[t], 1)
                        else:
                            pe.matmul(zb[t][:, 0:D + 2 * H], gT[:, 0, t * P:(t + 1) * P], w1x[:, 0, :], start=True, stop=False)
                            pe.matmul(zb[t][:, 0:D + 2 * H], gT[:, 1, t * P:(t + 1) * P], w1x[:, 1, :], start=False, stop=True)\
                              .then_inc(z_full[t], 1)
                if a in (2, 20):
                    l = (a - 2) // 18
                    pe.wait_ge(parts_ready, b * 2 + l + 1)
                    pe.wait_ge(t_free, t_value(b, l, 0))
                    pe.nop(nofuse=True)
                    for t in range(T):
                        mm = pe.transpose(tb[0:KZ, t * P // 2:(t + 1) * P // 2].bitcast(BF16),
                                          parts[:, t, :, :].rearrange("p a c -> p (a c)"), identb[:, :])
                    mm.then_inc(t_full, 1)
                for l in range(2):
                    k = a - 4 - 18 * l
                    if 0 <= k < NU:
                        if k == 0:
                            pe.wait_ge(pair_ready, b * 2 + l + 1)
                        t, hp = divmod(k, 4)
                        pe.wait_ge(z_free[k % 2], z_value(b, l, k // 2 + 1))
                        pe.matmul(zb[k % 2][:, :], pair_l[:, t * P:(t + 1) * P],
                                  pair_r[:, 2 * hp:2 * hp + 2, :].rearrange("k h m -> k (h m)"), start=True, stop=True)\
                          .then_inc(z_full[k % 2], 1)
                    k = a - 6 - 18 * l
                    if 0 <= k < NU:
                        pe.wait_ge(shifted, b * 2 * NU + l * NU + k + 1)
                        pe.wait_ge(t_free, t_value(b, l, k + 1))
                        for h in range(2):
                            for m in range(T):
                                mm = pe.transpose(tb[:, (h * T + m) * P:(h * T + m + 1) * P],
                                                  tt[:, k % 2, h, m * P:(m + 1) * P], ident)
                        mm.then_inc(t_full, 1)
                    k = a - 7 - 18 * l
                    if 0 <= k < NU:
                        t, hp = divmod(k, 4)
                        pe.wait_ge(t_free, t_value(b, l, k + 1) + 1)
                        if hp == 0:
                            pe.wait_ge(o_free, b * 2 * T + l * T + t + 1)
                        for h in range(2):
                            hh = 2 * hp + h
                            for m in range(T):
                                mm = pe.matmul(ob[:, hh * FE:(hh + 1) * FE], gpT[:, k % 2, h, m, :], feat[:, m, hh, :],
                                               start=(m == 0), stop=(m == T - 1))
                        mm.then_inc(pv_done, 1)
                if a in (17, 37):
                    l = 0 if a == 17 else 1
                    if l == 0:
                        pe.wait_ge(gres_ready, (b + 1) * T)
                    else:
                        pe.wait_ge(hn_ready, b + 1)
                    src = gres if l == 0 else hn
                    pe.wait_ge(t_free, t_value(b, l, 9))
                    for k in range(KT):
                        for t in range(T):
                            mm = pe.transpose(tb[:, (k * T + t) * P:(k * T + t + 1) * P], src[:, t, k * P:(k + 1) * P], ident)
                    mm.then_inc(t_full, 1)

            def fill(b, w):
                kind, n = w
                ps = bank_of(w)
                bk, turn = PLACE[w]
                if kind == "qkv" and n == 0:
                    pe.wait_ge(t_free, t_value(b, 1, 9) + 1)
                if kind == "turn":
                    pe.wait_ge(rot_ready, b * QU + n + 4)
                if kind == "score":
                    g, j = divmod(n, 3)
                    t = min(j, 1)
                    emptied_all(pe, b, [("turn", t), ("turn", 2 + 2 * g + t)])
                if kind == "probT":
                    pe.wait_ge(prob_ready, b * 3 * HKV + n + 1)
                if kind == "av":
                    g, t = divmod(n, 2)
                    emptied_all(pe, b, [("probT", 3 * g + j) for j in ([0] if t == 0 else [1, 2])])
                if kind == "oproj":
                    emptied_all(pe, b, [("av", 2 * g + n) for g in range(HKV)])
                if kind == "h2T":
                    pe.wait_ge(h2n_ready, b + 1)
                if kind == "gate":
                    emptied_all(pe, b, [("h2T", t) for t in range(T)])
                if kind == "mixT":
                    pe.wait_ge(mix_ready, b + 1)
                if kind == "mix":
                    emptied_all(pe, b, [("mixT", t) for t in range(T)])
                if kind == "down":
                    emptied_all(pe, b, [("mix", p) for p in range((JT + 1) // 2)])
                if kind in ("score", "av", "oproj", "gate", "mix", "down"):
                    pe.nop(nofuse=True)
                pe.wait_ge(free[bk], b * FILLS + turn + 1)

                if kind == "qkv":
                    c, t = (HKV, n) if n < 2 else (HKV + 1, n - 2) if n < 4 else divmod(n - 4, 2)
                    for k in range(KT):
                        mm = pe.matmul(ps[:, :], hT[:, k, t * P:(t + 1) * P], wqkv_sb[:, k, c * G * HD:(c + 1) * G * HD],
                                       start=(k == 0), stop=(k == KT - 1))
                elif kind == "turn":
                    for h in range(G):
                        mm = pe.transpose(ps[:, h * P:(h + 1) * P], rot[:, n % 4, h * HD:(h + 1) * HD], ident)
                elif kind == "score":
                    nk = P * (t + 1)
                    heads = range(G) if t == 0 else range(2 * (j - 1), 2 * (j - 1) + 2)
                    for i, h in enumerate(heads):
                        pe.matmul(ps[:, i * nk:(i + 1) * nk], qT[:, G * g + h, t * P:(t + 1) * P], kT[:, g, 0:nk],
                                  start=True, stop=False)
                        mm = pe.matmul(ps[:, (i + 1) * nk - P:(i + 1) * nk], identb[:, :], causal[:, :], start=False, stop=True)
                elif kind == "probT":
                    g, j = divmod(n, 3)
                    if j == 0:
                        for h in range(G):
                            mm = pe.transpose(ps[:, h * P:(h + 1) * P], prob[:, n % 6, h * P:(h + 1) * P], ident)
                    else:
                        for m in range(T):
                            for h in range(2):
                                mm = pe.transpose(ps[:, (m * 2 + h) * P:(m * 2 + h + 1) * P],
                                                  prob[:, n % 6, h * N + m * P:h * N + (m + 1) * P], ident)
                elif kind == "av":
                    if t == 0:
                        mm = pe.matmul(ps[:, :], v_sb[:, 0, g * HD:(g + 1) * HD], pT0[:, :, :].rearrange("p h q -> p (h q)"),
                                       start=True, stop=True)
                    else:
                        for m in range(T):
                            mm = pe.matmul(ps[:, :], v_sb[:, m, g * HD:(g + 1) * HD],
                                           pT1[:, m, :, :].rearrange("p h q -> p (h q)"), start=(m == 0), stop=(m == T - 1))
                elif kind == "oproj":
                    for h in range(HQ):
                        mm = pe.matmul(ps[:, 0:D], oT[:, h, n * P:(n + 1) * P], wo_sb[:, h, :], start=(h == 0), stop=(h == HQ - 1))
                elif kind == "h2T":
                    for k in range(KT):
                        mm = pe.transpose(ps[:, k * P:(k + 1) * P], h2n[:, n, k * P:(k + 1) * P], ident)
                elif kind == "gate":
                    for t in range(T):
                        for k in range(KT):
                            mm = pe.matmul(ps[:, t * E:(t + 1) * E], tokT[:, k, t * P:(t + 1) * P], wgate_sb[:, k, :],
                                           start=(k == 0), stop=(k == KT - 1))
                elif kind == "updown":
                    for m in range(2):
                        for k in range(KT):
                            mm = pe.matmul(ps[:, m * N:(m + 1) * N], wgu_sb[:, m, k, n * P:(n + 1) * P], tokT[:, k, :],
                                           start=(k == 0), stop=(k == KT - 1))
                elif kind == "mixT":
                    mm = pe.transpose(ps[0:NP * E, 0:P // 2].bitcast(BF16), mixp[:, n, :, :].rearrange("p a e -> p (a e)"), identb[:, :])
                elif kind == "mix":
                    for i, j in enumerate(range(2 * n, min(2 * n + 2, JT))):
                        mm = pe.matmul(ps[:, i * N:(i + 1) * N], expert_rows[:, j * P:(j + 1) * P], mixT[:, :], start=True, stop=True)
                elif kind == "down":
                    for j in range(JT):
                        mm = pe.matmul(ps[:, 0:D], ah[:, j, n * P:(n + 1) * P], wd_sb[:, j, :], start=(j == 0), stop=(j == JT - 1))
                mm.then_inc(full[bk], 1)

            pe.wait_ge(in_cst, 32)
            pe.wait_ge(setup_done, 1)
            for s in range(STEPS):
                gat(0, s)
            pe.wait_ge(in_qkv, 16)
            pe.wait_ge(in_o, 16)
            pe.wait_ge(in_gu, 48)
            pe.wait_ge(in_d, 16)
            with pe.Fori(0, B - 1) as b:
                for s in range(STEPS):
                    for w in work(s):
                        fill(b, w)
                    gat(b + 1, s)
            for s in range(STEPS):
                for w in work(s):
                    fill(B - 1, w)

        @block.scalar
        def _(act):
            def gat(b, a):
                if a in (1, 19):
                    l = (a - 1) // 18
                    for t in range(T):
                        act.wait_ge(z_full[t], z_value(b, l, 0))
                        act.activation(feat[:, t, :, 0:FO], zb[t][:, 0:D].rearrange("p (h o) -> p h o", h=H), ACT.Copy)\
                           .then_inc(z_free[t], 1)
                for l in range(2):
                    k = a - 4 - 18 * l
                    if 0 <= k < NU:
                        act.wait_ge(z_full[k % 2], z_value(b, l, k // 2 + 1))
                        act.wait_ge(lrelu_done, b * 2 * NU + l * NU + k + 1)
                        act.activation(zs[:, k % 2, :], zb[k % 2][:, :], ACT.Copy).then_inc(z_free[k % 2], 1)
                    k = a - 6 - 18 * l
                    if 0 <= k < NU:
                        act.wait_ge(t_full, t_value(b, l, k + 1))
                        if k >= 2:
                            act.wait_ge(pv_done, b * 2 * NU + l * NU + k - 1)
                        act.activation(gpT[:, k % 2, :, :, :].rearrange("p h m i -> p (h m i)"), tb[:, :], ACT.Exp).then_inc(t_free, 1)
                for l in range(2):
                    for t in range(T):
                        if a == 10 + 4 * t + 18 * l + 1:
                            act.wait_ge(gout_ready, b * 2 * T + l * T + t + 1)
                            act.activation(gex[:, t, :], go[:, t, :], ACT.Exp).then_inc(gexp_ready, 1)

            def empty(b, w):
                kind, n = w
                ps = bank_of(w)
                if kind == "qkv":
                    filled(act, b, w)
                    if n in (2, 3):
                        act.activation(v_sb[:, n - 2, :], ps[:, :], ACT.Copy).then_inc(free_of(w), 1)
                    else:
                        u = n if n < 2 else n - 2
                        act.wait_ge(rot_ready, b * QU + u + 1)
                        act.activation(raw[:, u % 3, :], ps[:, :], ACT.Copy).then_inc(raw_ready, 1)
                        act.activation(sq[:, u % 3, :], ps[:, :], ACT.Square).then_inc(free_of(w), 1)
                elif kind == "turn":
                    filled(act, b, w)
                    if n < 2:
                        dst = kT[:, :, n * P:(n + 1) * P]
                    else:
                        g, t = divmod(n - 2, 2)
                        dst = qT[:, G * g:G * g + G, t * P:(t + 1) * P]
                    act.activation(dst, ps[:, :].rearrange("p (h q) -> p h q", h=G), ACT.Copy).then_inc(free_of(w), 1)
                elif kind == "score":
                    g, j = divmod(n, 3)
                    t = min(j, 1)
                    nk = P * (t + 1)
                    heads = range(G) if t == 0 else range(2 * (j - 1), 2 * (j - 1) + 2)
                    act.wait_ge(sneg_ready, b * 3 * HKV + n + 1)
                    if n >= 6:
                        filled(act, b, ("probT", n - 6))
                    for i, h in enumerate(heads):
                        ins = act.activation(prob[:, n % 6, i * nk:(i + 1) * nk], ps[:, i * nk:(i + 1) * nk], ACT.Exp,
                                             bias=sneg[:, n, i:i + 1], scale=rq[:, g, t, h:h + 1], accum_out=ssum[:, n, i:i + 1])
                    ins.then_inc(free_of(w), 1)
                elif kind == "av":
                    g, t = divmod(n, 2)
                    filled(act, b, w)
                    act.activation(oT[:, G * g:G * g + G, t * P:(t + 1) * P], ps[:, :].rearrange("p (h q) -> p h q", h=G), ACT.Copy)\
                       .then_inc(free_of(w), 1)
                elif kind == "gate":
                    for t in range(T):
                        act.wait_ge(lneg_ready, b * T + t + 1)
                        act.activation(lex[:, t, :], lg[:, t, :], ACT.Exp, bias=lmx[:, t:t + 1]).then_inc(lexp_ready, 1)
                elif kind == "updown":
                    filled(act, b, w)
                    if n >= 3:
                        emptied(act, b, ("updown", n - 3))
                    act.activation(th[:, n % 3, :], ps[:, 0:N], ACT.Tanh, scale=0.5).then_inc(tanh_ready, 1)

            for s in range(STEPS):
                gat(0, s)
            with act.Fori(0, B - 1) as b:
                for s in range(STEPS):
                    for w in work(s):
                        empty(b, w)
                    gat(b + 1, s)
            for s in range(STEPS):
                for w in work(s):
                    empty(B - 1, w)

        @block.gpsimd
        def _(pool):
            def gat(b, a):
                for l in range(2):
                    k = a - 5 - 18 * l
                    if 0 <= k < NU:
                        pool.wait_ge(score_ready, b * 2 * NU + l * NU + k + 1)
                        pool.nop(nofuse=True)
                        for h in range(2):
                            ins = pool.tensor_scalar(tt[:, k % 2, h, :], tt[:, k % 2, h, :], gneg[:, k % 2, h:h + 1], 1.0,
                                                     ALU.add, ALU.mult)
                        ins.then_inc(shifted, 1)

            def part(b, w):
                kind, n = w
                if kind == "qkv" and n not in (2, 3):
                    u = n if n < 2 else n - 2
                    which, t = (1, u) if u < 2 else (0, u % 2)
                    pool.wait_ge(raw_ready, b * QU + u + 1)
                    pool.wait_ge(rot_ready, b * QU + u + 2)
                    src = raw[:, u % 3, :].rearrange("p (h c d) -> p h c d", h=G, c=2)
                    dst = m2[:, u % 2, :].rearrange("p (h c d) -> p h c d", h=G, c=2)
                    for c in range(2):
                        s_ = rope_s[:, which, t, c * HD // 2:(c + 1) * HD // 2].unsqueeze(1).broadcast_to([P, G, HD // 2])
                        ins = pool.tensor_tensor(dst[:, :, c, :], src[:, :, 1 - c, :], s_, ALU.mult)
                    ins.then_inc(m2_ready, 1)
                elif kind == "oproj":
                    pool.wait_ge(hid2_ready, b * T + n + 1)
                    pool.tensor_tensor(osum[:, n, :], x1[:, n, :], hid2[:, n, :], ALU.add).then_inc(osum_ready, 1)

            def normalise(b, s):
                for n in summed(s):
                    nh, nk = (G, P) if n % 3 == 0 else (2, N)
                    pool.wait_ge(srcp_ready, b * 3 * HKV + n + 1)
                    pool.nop(nofuse=True)
                    for i in range(nh):
                        part_ = prob[:, n % 6, i * nk:(i + 1) * nk]
                        ins = pool.tensor_scalar(part_, part_, srcp[:, n, i:i + 1], 1.0, ALU.mult, ALU.mult)
                    ins.then_inc(prob_ready, 1)

            pool.wait_ge(setup_done, 1)
            for s in range(STEPS):
                gat(0, s)
            with pool.Fori(0, B - 1) as b:
                for s in range(STEPS):
                    for w in work(s):
                        part(b, w)
                    normalise(b, s)
                    gat(b + 1, s)
            for s in range(STEPS):
                for w in work(s):
                    part(B - 1, w)
                normalise(B - 1, s)

        A_LINKS, B_LINKS = [0], [0]

        @block.vector
        def _(dve):
            count = [0, 0]

            def link_a(b, ins):
                count[0] += 1
                ins.then_inc(dve_a, 1)
                dve.wait_ge(dve_a, b * N_A + count[0])

            def link_b(b, ins):
                count[1] += 1
                ins.then_inc(dve_b, 1)
                dve.wait_ge(dve_b, b * N_B + count[1])

            def rsqrt(link, b, y, a, v):
                link(b, dve.tensor_scalar(a.bitcast(I32), v.bitcast(I32), 1, None, ALU.logical_shift_right))
                link(b, dve.tensor_scalar(y.bitcast(I32), a.bitcast(I32), -1, MAGIC, ALU.mult, ALU.add))
                for _ in range(3):
                    link(b, dve.scalar_tensor_tensor(a, y, -0.5, y, ALU.mult, ALU.mult))
                    link(b, dve.tensor_tensor(a, a, v, ALU.mult))
                    link(b, dve.scalar_tensor_tensor(y, a, 1.5, y, ALU.add, ALU.mult))

            def moments(b, src):
                for t in range(T):
                    link_a(b, dve.bn_stats(stats[:, t, :], src[:, t, :]))
                    dve.nop(nofuse=True)
                    link_a(b, dve.bn_aggr(mv[:, t, :], stats[:, t, :]))

            def gat(b, a):
                if a == 0:
                    dve.wait_ge(in_x, (b + 1) * 16)
                    moments(b, xin)
                    link_a(b, dve.tensor_scalar(rs_v[:, 0:T], mv[:, :, 1], LN_EPS, None, ALU.add))
                    rsqrt(link_a, b, rs_y[:, 0:T], rs_a[:, 0:T], rs_v[:, 0:T])
                    for t in range(T):
                        link_a(b, dve.tensor_scalar(maskv[:, t, :], xin[:, t, :], mv[:, t, 0:1], rs_y[:, t:t + 1],
                                                    ALU.subtract, ALU.mult))
                        link_a(b, dve.tensor_scalar(maskv[:, t, :], maskv[:, t, :], 1.0, 1e10, ALU.subtract, ALU.mult))
                if a in (1, 19):
                    l = (a - 1) // 18
                    for t in range(T):
                        dve.wait_ge(z_free[t], z_value(b, l, 0) + 1)
                        ps = zb[t][:, D:D + 2 * H]
                        link_a(b, dve.tensor_copy(parts[:, t, 0, :], ps))
                        link_a(b, dve.tensor_tensor(sn_res[:, t, :], ps, parts[:, t, 0, :], ALU.subtract))
                        link_a(b, dve.tensor_copy(parts[:, t, 1, :], sn_res[:, t, :]))
                        ins = dve.tensor_tensor(parts[:, t, 2, :], sn_res[:, t, :], parts[:, t, 1, :], ALU.subtract)
                    ins.then_inc(parts_ready, 1)
                    if l == 0:
                        dve.sem_inc(c_used, 1)
                if a in (2, 20):
                    l = (a - 2) // 18
                    dve.wait_ge(t_full, t_value(b, l, 0))
                    link_a(b, dve.tensor_copy(partsT[:, :], tb[0:KZ, 0:N // 2].bitcast(BF16)))
                    dve.tensor_scalar(pair_l[:, :], partsT[:, :], cst[0:KZ, C_SELF:C_SELF + 1], cst[0:KZ, C_NEIGH:C_NEIGH + 1],
                                      ALU.mult, ALU.add).then_inc(t_free, 1)
                    for h in range(H):
                        ins = dve.tensor_scalar(pair_r[:, h, :], partsT[:, :], cst[0:KZ, C_PICK + h:C_PICK + h + 1],
                                                cst[0:KZ, C_ONE + h:C_ONE + h + 1], ALU.mult, ALU.add)
                    ins.then_inc(pair_ready, 1)
                for l in range(2):
                    k = a - 4 - 18 * l
                    if 0 <= k < NU:
                        t, hp = divmod(k, 4)
                        dve.wait_ge(z_free[k % 2], z_value(b, l, k // 2 + 1) + 1)
                        dve.scalar_tensor_tensor(lr[:, :], zs[:, k % 2, :], 0.2, zs[:, k % 2, :], ALU.mult, ALU.max)\
                           .then_inc(lrelu_done, 1)
                        dve.wait_ge(lrelu_done, b * 2 * NU + l * NU + k + 3)
                        if k >= 2:
                            dve.wait_ge(t_full, t_value(b, l, k - 1))
                        dve.nop(nofuse=True)
                        for h in range(2):
                            ins = dve.tensor_tensor_reduce(tt[:, k % 2, h, :], lr[:, h * N:(h + 1) * N], maskv[:, t, :], 1.0, -3e38,
                                                           ALU.add, ALU.max, gmx[:, k % 2, h:h + 1])
                        link_a(b, ins)
                        dve.tensor_scalar(gneg[:, k % 2, :], gmx[:, k % 2, :], -1.0, None, ALU.mult).then_inc(score_ready, 1)
                for l in range(2):
                    for t in range(T):
                        if a == 10 + 4 * t + 18 * l:
                            dve.wait_ge(pv_done, b * 2 * NU + l * NU + 4 * t + 4)
                            o_ = ob[:, 0:H * FE].rearrange("p (h o) -> p h o", h=H)
                            link_a(b, dve.reciprocal(gsum[:, :], o_[:, :, FO]))
                            g_ = go[:, t, :].rearrange("p (h o) -> p h o", h=H)
                            ins = dve.tensor_tensor(g_, o_[:, :, 0:FO], gsum[:, :].unsqueeze(2).broadcast_to([P, H, FO]), ALU.mult)
                            ins.then_inc(o_free, 1)
                            dve.wait_ge(o_free, b * 2 * T + l * T + t + 2)
                            dve.tensor_tensor(go[:, t, :], go[:, t, :], rows[:, (3 * l + 2) * D:(3 * l + 3) * D], ALU.add)\
                               .then_inc(gout_ready, 1)
                        if a == 10 + 4 * t + 18 * l + 1:
                            dve.wait_ge(gexp_ready, b * 2 * T + l * T + t + 1)
                            link_a(b, dve.tensor_scalar(gex[:, t, :], gex[:, t, :], 1.0, -1.0, ALU.min, ALU.add))
                            ins = dve.scalar_tensor_tensor(gres[:, t, :], go[:, t, :], 0.0, gex[:, t, :], ALU.max, ALU.add)
                            if l == 0:
                                ins.then_inc(gres_ready, 1)
                            else:
                                link_a(b, ins)
                                link_a(b, dve.tensor_tensor(x1[:, t, :], xin[:, t, :], gres[:, t, :], ALU.add))
                                if t == T - 1:
                                    dve.sem_inc(x_used, 1)
                if a == 17:
                    dve.wait_ge(t_full, t_value(b, 0, 9))
                    dve.tensor_copy(gT[:, :, :].rearrange("p k n -> p (k n)"), tb[:, :]).then_inc(t_free, 1)
                if a == 35:
                    moments(b, x1)
                    link_a(b, dve.tensor_scalar(rs_v[:, 0:T], mv[:, :, 1], LN_EPS, None, ALU.add))
                    link_a(b, dve.scalar_tensor_tensor(rs_v[:, T:2 * T], rs_v[:, 0:T], RMS_EPS, mv[:, :, 1], ALU.mult, ALU.add))
                    rsqrt(link_a, b, rs_y[:, :], rs_a[:, :], rs_v[:, :])
                    for t in range(T):
                        link_a(b, dve.tensor_scalar(hid[:, t, :], x1[:, t, :], mv[:, t, 0:1], rs_y[:, t:t + 1],
                                                    ALU.subtract, ALU.mult))
                        ins = dve.tensor_scalar(hn[:, t, :], x1[:, t, :], mv[:, t, 0:1], rs_y[:, T + t:T + t + 1],
                                                ALU.subtract, ALU.mult)
                    ins.then_inc(hn_ready, 1)
                if a == 37:
                    dve.wait_ge(t_full, t_value(b, 1, 9))
                    for k in range(KT):
                        ins = dve.tensor_scalar(hT[:, k, :], tb[:, k * N:(k + 1) * N], cols[:, k:k + 1], None, ALU.mult)
                    ins.then_inc(t_free, 1)

            def part(b, w):
                kind, n = w
                ps = bank_of(w)
                if kind == "qkv" and n not in (2, 3):
                    u = n if n < 2 else n - 2
                    which, t = (1, u) if u < 2 else (0, u % 2)
                    emptied(dve, b, w)
                    link_b(b, dve.tensor_reduce(ssq[:, u, :], sq[:, u % 3, :].rearrange("p (h d) -> p h d", h=G), AX.X, ALU.add))
                    if t == 1:
                        link_b(b, dve.tensor_scalar(qk_v[:, :], ssq[:, u - 1:u + 1, :].rearrange("p a h -> p (a h)"), 1.0 / HD, RMS_EPS,
                                                    ALU.mult, ALU.add))
                        rsqrt(link_b, b, qk_y[:, :], qk_a[:, :], qk_v[:, :])
                        if which == 1:
                            link_b(b, dve.tensor_copy(rk[:, :, :].rearrange("p t h -> p (t h)"), qk_y[:, :]))
                        else:
                            g = (u - 2) // 2
                            link_b(b, dve.tensor_scalar(rq[:, g, :, :].rearrange("p t h -> p (t h)"), qk_y[:, :], SCALE, None, ALU.mult))
                    for v in ([] if u == 0 else [0, 1] if u == 1 else [u]):
                        tv = v % 2
                        if v >= 4:
                            filled(dve, b, ("turn", v - 4))
                        dve.wait_ge(raw_ready, b * QU + v + 1)
                        c_ = rope_c[:, which, tv, :].unsqueeze(1).broadcast_to([P, G, HD])
                        link_b(b, dve.tensor_tensor(m1[:, :].rearrange("p (h d) -> p h d", h=G),
                                                    raw[:, v % 3, :].rearrange("p (h d) -> p h d", h=G), c_, ALU.mult))
                        dve.wait_ge(m2_ready, b * QU + v + 1)
                        ins = dve.tensor_tensor(rot[:, v % 4, :], m1[:, :], m2[:, v % 2, :], ALU.add)
                        if which == 1:
                            link_b(b, ins)
                            r_ = rot[:, v % 4, :].rearrange("p (h d) -> p h d", h=G)
                            ins = dve.tensor_tensor(r_, r_, rk[:, tv, :].unsqueeze(2).broadcast_to([P, G, HD]), ALU.mult)
                        ins.then_inc(rot_ready, 1)
                        dve.wait_ge(rot_ready, b * QU + v + 4)
                elif kind == "score":
                    g, j = divmod(n, 3)
                    t = min(j, 1)
                    nh, nk = (G, P) if j == 0 else (2, N)
                    h0 = 0 if j == 0 else 2 * (j - 1)
                    filled(dve, b, w)
                    link_b(b, dve.tensor_reduce(smx[:, n, 0:nh], ps[:, :].rearrange("p (h k) -> p h k", h=nh), AX.X, ALU.max))
                    dve.scalar_tensor_tensor(sneg[:, n, 0:nh], smx[:, n, 0:nh], -1.0, rq[:, g, t, h0:h0 + nh], ALU.mult, ALU.mult)\
                       .then_inc(sneg_ready, 1)
                elif kind == "probT":
                    g, j = divmod(n, 3)
                    filled(dve, b, w)
                    if j == 0:
                        if g:
                            filled(dve, b, ("av", 2 * (g - 1)))
                        dve.tensor_copy(pT0[:, :, :].rearrange("p h q -> p (h q)"), ps[:, :]).then_inc(free_of(w), 1)
                    else:
                        if g:
                            filled(dve, b, ("av", 2 * (g - 1) + 1))
                        dve.tensor_copy(pT1[:, :, 2 * (j - 1):2 * j, :], ps[:, :].rearrange("p (m h q) -> p m h q", m=T, h=2))\
                           .then_inc(free_of(w), 1)
                elif kind == "oproj":
                    filled(dve, b, w)
                    dve.tensor_tensor(hid2[:, n, :], ps[:, 0:D], hid[:, n, :], ALU.add).then_inc(free_of(w), 1)
                    emptied(dve, b, w)
                    dve.tensor_tensor_reduce(h2n[:, n, :], hid2[:, n, :], hid2[:, n, :], 1.0, 0.0, ALU.mult, ALU.add, ss2[:, n:n + 1])\
                       .then_inc(hid2_ready, 1)
                    if n == T - 1:
                        dve.wait_ge(hid2_ready, (b + 1) * T)
                        link_b(b, dve.tensor_scalar(qk_v[:, 0:T], ss2[:, :], 1.0 / D, RMS_EPS, ALU.mult, ALU.add))
                        rsqrt(link_b, b, qk_y[:, 0:T], qk_a[:, 0:T], qk_v[:, 0:T])
                        for t in range(T):
                            ins = dve.tensor_scalar(h2n[:, t, :], hid2[:, t, :], qk_y[:, t:t + 1], None, ALU.mult)
                        ins.then_inc(h2n_ready, 1)
                elif kind == "h2T":
                    filled(dve, b, w)
                    for k in range(KT):
                        ins = dve.tensor_scalar(tokT[:, k, n * P:(n + 1) * P], ps[:, k * P:(k + 1) * P], cols[:, KT + k:KT + k + 1], None,
                                                ALU.mult)
                    ins.then_inc(free_of(w), 1)
                elif kind == "gate":
                    filled(dve, b, w)
                    link_b(b, dve.tensor_copy(lg[:, :, :].rearrange("p t e -> p (t e)"), ps[:, 0:T * E]))
                    ins = dve.tensor_reduce(lmx[:, :], lg[:, :, :], AX.X, ALU.max)
                    ins.then_inc(free_of(w), 1)
                    emptied(dve, b, w)
                    for t in range(T):
                        dve.tensor_scalar(lmx[:, t:t + 1], lmx[:, t:t + 1], -1.0, None, ALU.mult).then_inc(lneg_ready, 1)
                elif kind == "updown":
                    if n == 0:
                        dve.wait_ge(osum_ready, (b + 1) * T)
                    if n == 1:
                        mixing(b)
                    dve.wait_ge(tanh_ready, b * JT + n + 1)
                    link_b(b, dve.scalar_tensor_tensor(ga[:, :], th[:, n % 3, :], 1.0, ps[:, 0:N], ALU.add, ALU.mult))
                    dve.scalar_tensor_tensor(ah[:, n, :], ga[:, :], 0.5, ps[:, N:2 * N], ALU.mult, ALU.mult).then_inc(free_of(w), 1)
                    emptied(dve, b, w)
                elif kind == "mixT":
                    filled(dve, b, w)
                    dve.tensor_copy(mixT[:, n * P:(n + 1) * P], ps[0:NP * E, 0:P // 2].bitcast(BF16)).then_inc(free_of(w), 1)
                elif kind == "mix":
                    filled(dve, b, w)
                    j0, j1 = 2 * n, min(2 * n + 2, JT)
                    a_ = ah[:, j0:j1, :].rearrange("p j n -> p (j n)")
                    dve.tensor_tensor(a_, a_, ps[:, 0:(j1 - j0) * N], ALU.mult).then_inc(free_of(w), 1)
                elif kind == "down":
                    filled(dve, b, w)
                    dve.wait_ge(osum_ready, b * T + n + 1)
                    dve.wait_ge(out_free, (b + 1) * 16 * T)
                    dve.tensor_tensor(yo[:, n, :], osum[:, n, :], ps[:, 0:D], ALU.add).then_inc(free_of(w), 1)
                    emptied(dve, b, w)
                    dve.sem_inc(y_ready, 1)

            def reciprocals(b, s):
                for n in summed(s):
                    nh = G if n % 3 == 0 else 2
                    emptied(dve, b, ("score", n))
                    dve.reciprocal(srcp[:, n, 0:nh], ssum[:, n, 0:nh]).then_inc(srcp_ready, 1)

            def mixing(b):
                dve.wait_ge(lexp_ready, (b + 1) * T)
                link_b(b, dve.tensor_reduce(lmx[:, :], lex[:, :, :], AX.X, ALU.add))
                link_b(b, dve.reciprocal(lmx[:, :], lmx[:, :]))
                link_b(b, dve.tensor_tensor(lex[:, :, :], lex[:, :, :], lmx[:, :].unsqueeze(2).broadcast_to([P, T, E]), ALU.mult))
                tri = cst[:, C_TRI:C_TRI + E * E].rearrange("p (e j) -> p e j", e=E)
                for t in range(T):
                    mine = lex[:, t, :].unsqueeze(2).broadcast_to([P, E, E])
                    other = lex[:, t, :].unsqueeze(1).broadcast_to([P, E, E])
                    link_b(b, dve.tensor_tensor(cmp1[:, t, :, :], other, mine, ALU.is_gt))
                    link_b(b, dve.tensor_tensor(cmp2[:, t, :, :], other, mine, ALU.is_equal))
                    link_b(b, dve.tensor_tensor(cmp2[:, t, :, :], cmp2[:, t, :, :], tri, ALU.mult))
                    link_b(b, dve.tensor_tensor(cmp1[:, t, :, :], cmp1[:, t, :, :], cmp2[:, t, :, :], ALU.add))
                link_b(b, dve.tensor_reduce(rank[:, :, :], cmp1[:, :, :, :], AX.X, ALU.add))
                link_b(b, dve.scalar_tensor_tensor(lex[:, :, :], rank[:, :, :], 2.0, lex[:, :, :], ALU.is_lt, ALU.mult))
                link_b(b, dve.tensor_reduce(lmx[:, :], lex[:, :, :], AX.X, ALU.add))
                link_b(b, dve.tensor_scalar(lmx[:, :], lmx[:, :], 1e-9, None, ALU.add))
                link_b(b, dve.reciprocal(lmx[:, :], lmx[:, :]))
                link_b(b, dve.tensor_tensor(lex[:, :, :], lex[:, :, :], lmx[:, :].unsqueeze(2).broadcast_to([P, T, E]), ALU.mult))
                link_b(b, dve.tensor_copy(mixp[:, :, 0, :], lex[:, :, :]))
                link_b(b, dve.tensor_tensor(rank[:, :, :], lex[:, :, :], mixp[:, :, 0, :], ALU.subtract))
                link_b(b, dve.tensor_copy(mixp[:, :, 1, :], rank[:, :, :]))
                dve.tensor_tensor(mixp[:, :, 2, :], rank[:, :, :], mixp[:, :, 1, :], ALU.subtract).then_inc(mix_ready, 1)

            n_setup = [0]

            def link(ins):
                n_setup[0] += 1
                ins.then_inc(setup_v, 1)
                dve.wait_ge(setup_v, n_setup[0])

            dve.wait_ge(in_cst, 32)
            link(dve.tensor_copy(identb[:, :], ident))
            link(dve.tensor_copy(causal[:, :], cst[:, C_CAUSAL:C_CAUSAL + P]))
            link(dve.tensor_copy(expert_rows[:, :], spread_in))
            for t in range(T):
                link(dve.memset(feat[:, t, :, FO:FE], 1.0))
            dve.wait_ge(in_gat, 80)
            for l in range(2):
                for k in range(1 if l == 0 else KT):
                    wx = w0x[:, :] if l == 0 else w1x[:, k, :]
                    np_ = F_IN if l == 0 else P
                    for v in range(2):
                        link(dve.tensor_tensor(wprod[0:np_, :], wx[:, 0:D], rows[0:np_, (3 * l + v) * D:(3 * l + v + 1) * D], ALU.mult))
                        link(dve.tensor_reduce(wx[:, D + v * H:D + (v + 1) * H], wprod[0:np_, :].rearrange("p (h o) -> p h o", h=H),
                                               AX.X, ALU.add))
            for m in range(2):
                for t in range(T):
                    w_ = qkw[:, m * HD:(m + 1) * HD]
                    link(dve.tensor_tensor(rope_c[:, m, t, :], cst[:, C_COS + t * HD:C_COS + (t + 1) * HD], w_, ALU.mult))
                    for c in range(2):
                        half = slice(c * HD // 2, (c + 1) * HD // 2)
                        link(dve.tensor_tensor(rope_s[:, m, t, half], cst[:, C_SIN + t * HD + c * HD // 2:C_SIN + t * HD + (c + 1) * HD // 2],
                                               qkw[:, m * HD + (1 - c) * HD // 2:m * HD + (2 - c) * HD // 2], ALU.mult))
            for k in range(2):
                dve.sem_inc(z_free[k], 1)
            dve.sem_inc(t_free, 1)
            dve.sem_inc(o_free, 1)
            dve.sem_inc(lrelu_done, 2)
            dve.sem_inc(rot_ready, 3)
            dve.sem_inc(out_free, 16 * T)
            for k in range(BANKS):
                dve.sem_inc(free[k], 1)
            dve.sem_inc(setup_done, 1)
            for s in range(STEPS):
                gat(0, s)
            assert count[0] == N_A, count
            with dve.Fori(0, B - 1) as b:
                count[:] = [0, 0]
                for s in range(STEPS):
                    for w in work(s):
                        part(b, w)
                    reciprocals(b, s)
                    gat(b + 1, s)
            assert count[1] == N_B, count
            count[:] = [0, 0]
            for s in range(STEPS):
                for w in work(s):
                    part(B - 1, w)
                reciprocals(B - 1, s)


def kernel(**inputs):
    import numpy as _np
    import concourse.bacc as _bacc
    from concourse import mybir as _mybir
    from concourse.bass_utils import run_bass_kernel_spmd as _run

    i = {k: _np.asarray(v) for k, v in inputs.items()}
    g = {k[len("L0_xattn_"):]: v for k, v in i.items() if k.startswith("L0_xattn_")}
    f = {k[len("L0_ffn_"):]: v for k, v in i.items() if k.startswith("L0_ffn_")}

    def on_rows(*vectors):
        return _np.concatenate([_np.broadcast_to(v.reshape(1, -1), (P, v.size)) for v in vectors], 1)

    arrays = {
        "x": i["x"],
        "ctxT": i["ctx_512"].transpose(0, 2, 1),
        "w0": g["W0"].transpose(1, 0, 2).reshape(F_IN, D),
        "w1": g["W1"].transpose(1, 0, 2).reshape(D, D),
        "gat_rows": on_rows(g["a_self0"], g["a_neigh0"], g["b0"], g["a_self1"], g["a_neigh1"], g["b1"]),
        "norm_cols": _np.concatenate([f["attn_norm_w"].reshape(KT, P).T, f["ffn_norm_w"].reshape(KT, P).T], 1),
        "qk_rows": on_rows(f["q_norm_w"], f["k_norm_w"]),
        "wqkv": _np.concatenate([f["q_w"], f["k_w"], f["v_w"]], 0).T,
        "wo": f["o_w"].T,
        "wgate": f["gate_w"].T,
        "wgu": _np.stack([f["wg"].reshape(EI, D).T, f["wu"].reshape(EI, D).T]),
        "wd": f["wd"].transpose(0, 2, 1).reshape(EI, D),
        "consts": constants()[0],
        "spread": constants()[1],
    }
    arrays = {k + "_dram": _np.ascontiguousarray(v) for k, v in arrays.items()}
    nc = _bacc.Bacc("TRN2", target_bir_lowering=False, num_devices=1)
    args = [nc.dram_tensor(k, v.shape, _mybir.dt.from_np(v.dtype), kind="ExternalInput").ap() for k, v in arrays.items()]
    args.append(nc.dram_tensor("out_dram", (B, N, D), _mybir.dt.float32, kind="ExternalOutput").ap())
    block_program(nc, *args)
    r = _run(nc, [arrays], core_ids=[0])
    return r.results[0]["out_dram"]
```

```python
import concourse.bass as bass
from concourse import mybir
from contextlib import ExitStack
import numpy as np

F32 = mybir.dt.float32
I32 = mybir.dt.int32
BF16 = mybir.dt.bfloat16
ALU = mybir.AluOpType
ACT = mybir.ActivationFunctionType
AX = mybir.AxisListType

P = 128
B, N, D = 4, 256, 256
T = N // P
KT = D // P
F_IN = 64
H, FO = 8, 32
FE = FO + 1
NP = 3
KZ = NP * 2 * H
HQ, HKV, HD = 16, 4, 128
G = HQ // HKV
E, I = 8, 176
EI = E * I
JT = EI // P
NU = 2 * T * 2
QU = (HQ + HKV) // G * T
LN_EPS, RMS_EPS = 1e-5, 1e-6
SCALE = float(HD) ** -0.5
MASKED = -1e30
MAGIC = 0x5F3759DF

C_ID = 0
C_CAUSAL = C_ID + P
C_COS = C_CAUSAL + P
C_SIN = C_COS + T * HD
C_PICK = C_SIN + T * HD
C_ONE = C_PICK + H
C_SELF = C_ONE + H
C_NEIGH = C_SELF + 1
C_TRI = C_NEIGH + 1
C_END = C_TRI + E * E


def constants():
    c = np.zeros((P, C_END), np.float32)
    c[:, C_ID:C_ID + P] = np.eye(P)
    c[:, C_CAUSAL:C_CAUSAL + P] = np.where(np.arange(P)[None, :] > np.arange(P)[:, None], MASKED, 0.0)
    freqs = (np.float32(1.0) / np.float32(1e6) ** (np.arange(0, HD, 2, dtype=np.float32) / np.float32(HD))).astype(np.float32)
    angle = np.outer(np.arange(N, dtype=np.float32), freqs).astype(np.float32)
    cos, sin = np.cos(angle), np.sin(angle)
    for t in range(T):
        rows = slice(t * P, (t + 1) * P)
        c[:, C_COS + t * HD:C_COS + (t + 1) * HD] = np.concatenate([cos[rows], cos[rows]], 1)
        c[:, C_SIN + t * HD:C_SIN + (t + 1) * HD] = np.concatenate([-sin[rows], sin[rows]], 1)
    for p in range(NP):
        for h in range(H):
            self_row, neigh_row = p * 2 * H + h, p * 2 * H + H + h
            c[neigh_row, C_PICK + h] = 1.0
            c[self_row, C_ONE + h] = 1.0
            c[self_row, C_SELF] = 1.0
            c[neigh_row, C_NEIGH] = 1.0
    for e in range(E):
        c[:, C_TRI + e * E:C_TRI + e * E + e] = 1.0
    spread = np.tile(np.repeat(np.eye(E, dtype=np.float32), I, axis=1), (NP, 1))
    return c, spread


N_A, N_B, N_P = 48, 75, 35

STEPS = 50
GAT = (1, 22)
Z_AT, TTR_AT, TURN_AT, PV_AT, OUT_AT = 5, 6, 8, 9, 18
LN2_AT, HN_AT = 40, 44
OPROJ, DOWN = 24, 46
O_PARTS, D_PARTS = 4, 2


def work(s):
    w = []
    if s < 12:
        w.append(("qkv", s))
    if 5 <= s < 5 + QU:
        w.append(("turn", s - 5))
    if 15 <= s < 15 + 2 * HKV:
        g, t = divmod(s - 15, 2)
        w += [("probT", 3 * g)] if t == 0 else [("probT", 3 * g + 1), ("probT", 3 * g + 2)]
    if 11 <= s < 11 + 2 * HKV:
        g, t = divmod(s - 11, 2)
        w += [("score", 3 * g)] if t == 0 else [("score", 3 * g + 1), ("score", 3 * g + 2)]
    if 16 <= s < 16 + 2 * HKV:
        w.append(("av", s - 16))
    if s in (OPROJ, OPROJ + O_PARTS):
        w.append(("oproj", (s - OPROJ) // O_PARTS))
    if s in (30, 34):
        w.append(("h2T", (s - 30) // 4))
    if s == 34:
        w.append(("gate", 0))
    if 34 <= s < 34 + JT:
        w.append(("updown", s - 34))
    if s == 38:
        w += [("mixT", 0), ("mixT", 1)]
    w += [("mix", p) for p, at in enumerate((40, 40, 41, 42, 44, 45)) if s == at]
    if s in (DOWN, DOWN + D_PARTS):
        w.append(("down", (s - DOWN) // D_PARTS))
    return w


def use(s):
    w = [x for x in work(s) if x[0] not in ("oproj", "down")]
    w += [x for x in work(s - O_PARTS + 1) if x[0] == "oproj"]
    w += [x for x in work(s - D_PARTS + 1) if x[0] == "down"]
    return w


def summed(s):
    return [n for kind, n in work(s - 2) if kind == "score"]


SLOW = ("score", "updown", "gate", "mixT")
SLOW_BANKS, QUICK_BANKS = 2, 3
BANKS = SLOW_BANKS + QUICK_BANKS
ORDER = [w for s in range(STEPS) for w in work(s)]
PLACE, FILLS = {}, {}
for first, banks, fills in ((0, SLOW_BANKS, [w for w in ORDER if w[0] in SLOW]),
                            (SLOW_BANKS, QUICK_BANKS, [w for w in ORDER if w[0] not in SLOW])):
    assert len(fills) % banks == 0
    for n, w in enumerate(fills):
        PLACE[w] = (first + n % banks, n // banks)
    for k in range(banks):
        FILLS[first + k] = len(fills) // banks


def block_program(nc, x, ctxT, w0, w1, gat_rows, norm_cols, qk_rows, wqkv, wo, wgate, wgu, wd, consts, spread, out):
    ctx = ExitStack()
    with ctx:
        def sb(name, shape, dt=F32):
            return ctx.enter_context(nc.sbuf_tensor(name, shape, dt))

        def pb(name, shape, dt=F32):
            return ctx.enter_context(nc.psum_tensor(name, shape, dt))

        def sem(name):
            return ctx.enter_context(nc.semaphore(name))

        cst = sb("cst", [P, C_END])
        ident = cst[:, C_ID:C_ID + P]
        identb = sb("identb", [P, P], BF16)
        causal = sb("causal", [P, P], BF16)
        expert_rows = sb("expert_rows", [NP * E, EI], BF16)
        rows = sb("rows", [P, 6 * D])
        w0x = sb("w0x", [F_IN, D + 2 * H])
        w1x = sb("w1x", [P, KT, D + 2 * H])
        cols = sb("cols", [P, 2 * KT])
        qkw = sb("qkw", [P, 2 * HD])
        rope_c = sb("rope_c", [P, 2, T, HD])
        rope_s = sb("rope_s", [P, 2, T, HD])
        wqkv_sb = sb("wqkv_sb", [P, KT, (HQ + 2 * HKV) * HD])
        wo_sb = sb("wo_sb", [P, HQ, D])
        wgate_sb = sb("wgate_sb", [P, KT, E])
        wgu_sb = sb("wgu_sb", [P, 2, KT, EI])
        wd_sb = sb("wd_sb", [P, JT, D])
        xin = sb("xin", [P, T, D])
        cin = sb("cin", [F_IN, N])
        stats = sb("stats", [P, T, 6])
        mv = sb("mv", [P, T, 2])
        rs_v = sb("rs_v", [P, 2 * T])
        rs_y = sb("rs_y", [P, 2 * T])
        rs_a = sb("rs_a", [P, 2 * T])
        maskv = sb("maskv", [P, T, N])
        feat = sb("feat", [P, T, H, FE])
        sn_res = sb("sn_res", [P, T, 2 * H])
        parts = sb("parts", [P, T, NP, 2 * H], BF16)
        partsT = sb("partsT", [KZ, N], BF16)
        pair_l = sb("pair_l", [KZ, N], BF16)
        pair_r = sb("pair_r", [KZ, H, N], BF16)
        zs = sb("zs", [P, 2, 2 * N])
        lr = sb("lr", [P, 2, 2 * N])
        tt = sb("tt", [P, 3, 2, N])
        gmn = sb("gmn", [P, 3, 2])
        gpT = sb("gpT", [P, 2, 2, T, P])
        gsum = sb("gsum", [P, H])
        go = sb("go", [P, T, D])
        wprod = go[:, 0, :]
        gex = sb("gex", [P, T, D])
        x1 = sb("x1", [P, T, D])
        hid = sb("hid", [P, T, D])
        hn = gex
        hT = sb("hT", [P, KT, N])
        gT = hT
        early = sb("early", [P, 6, G * HD])[:, :, :]
        raw, sq = early[:, 0:3, :], early[:, 3:6, :]
        v_sb = sb("v_sb", [P, T, HKV * HD])
        m1 = sb("m1", [P, 4, G * HD])
        m2 = sb("m2", [P, 4, G * HD])
        ssq = sb("ssq", [P, QU * G])
        rms = sb("rms", [P, QU * G])
        rms_a = sb("rms_a", [P, QU * G])
        h2_v = sb("h2_v", [P, T])
        h2_y = sb("h2_y", [P, T])
        h2_a = sb("h2_a", [P, T])
        qT = sb("qT", [P, HQ, N])
        kT = sb("kT", [P, HKV, N])
        smx = sb("smx", [P, 3 * HKV, G])
        sneg = sb("sneg", [P, 3 * HKV, G])
        ssum = sb("ssum", [P, 3 * HKV, G])
        srcp = sb("srcp", [P, 3 * HKV, G])
        prob = sb("prob", [P, 6, 2 * N])
        pT0 = sb("pT0", [P, G, P])
        pT1 = sb("pT1", [P, T, G, P])
        oT = qT
        late = m1[:, :, :].rearrange("p a (t d) -> p a t d", t=T)
        hid2, osum, h2n = late[:, 0], late[:, 1], late[:, 2]
        ss2 = sb("ss2", [P, T])
        tokT = late[:, 3]
        lg = sb("lg", [P, T, E])
        lmx = sb("lmx", [P, T])
        lex = sb("lex", [P, T, E])
        spare = pT0[:, :, :].rearrange("p h q -> p (h q)")
        cmp1 = spare[:, N:N + T * E * E].rearrange("p (t e j) -> p t e j", t=T, e=E)
        cmp2 = spare[:, N + T * E * E:N + 2 * T * E * E].rearrange("p (t e j) -> p t e j", t=T, e=E)
        rank = sb("rank", [P, T, E])
        mixp = sb("mixp", [P, T, NP, E], BF16)
        mixT = sb("mixT", [NP * E, N], BF16)
        th = pT1[:, :, :, :].rearrange("p m h q -> p (m h q)")[:, 0:3 * N].rearrange("p (a n) -> p a n", a=3)
        ga = spare[:, 0:N]
        ah = early.rearrange("p a c -> p (a c)")[:, 0:JT * N].rearrange("p (j n) -> p j n", j=JT)
        yo = rows[:, 0:T * D].rearrange("p (t d) -> p t d", t=T)
        spread_in = ah[0:NP * E, :, :].rearrange("p j n -> p (j n)")[:, 0:EI]

        zb = pb("zb", [P, 512])
        tb = pb("tb", [P, 512])
        ob = pb("ob", [P, 512])
        bank = [pb(f"bank{k}", [P, 512]) for k in range(BANKS)]

        in_cst, in_gat, in_x, in_c = sem("in_cst"), sem("in_gat"), sem("in_x"), sem("in_c")
        in_qkv, in_o, in_gu, in_d = sem("in_qkv"), sem("in_o"), sem("in_gu"), sem("in_d")
        out_free = sem("out_free")
        x_used, c_used = sem("x_used"), sem("c_used")
        setup_v, setup_done = sem("setup_v"), sem("setup_done")
        dve_a = sem("dve_a")
        z_full, z_free = sem("z_full"), sem("z_free")
        t_full, t_free = sem("t_full"), sem("t_free")
        parts_ready, pair_l_ready, pair_r_ready = sem("parts_ready"), sem("pair_l_ready"), sem("pair_r_ready")
        lrelu_done, score_ready, shifted = sem("lrelu_done"), sem("score_ready"), sem("shifted")
        pv_done, o_free = sem("pv_done"), sem("o_free")
        gout_ready, gexp_ready, gres_ready, hn_ready = sem("gout_ready"), sem("gexp_ready"), sem("gres_ready"), sem("hn_ready")
        dve_b = sem("dve_b")
        full = [sem(f"full{k}") for k in range(BANKS)]
        free = [sem(f"free{k}") for k in range(BANKS)]
        raw_ready, m1_ready, m2_ready = sem("raw_ready"), sem("m1_ready"), sem("m2_ready")
        k_ready, seed_ready, rms_ready, pool_b = sem("k_ready"), sem("seed_ready"), sem("rms_ready"), sem("pool_b")
        sneg_ready, srcp_ready, prob_ready = sem("sneg_ready"), sem("srcp_ready"), sem("prob_ready")
        hid2_ready, osum_ready, h2n_ready = sem("hid2_ready"), sem("osum_ready"), sem("h2n_ready")
        lneg_ready, lexp_ready, mix_ready, tanh_ready, y_ready = sem("lneg_ready"), sem("lexp_ready"), sem("mix_ready"), sem("tanh_ready"), sem("y_ready")

        block = ctx.enter_context(nc.Block())

        def z_value(b, l, n):
            return b * 2 * (NU + 1) + l * (NU + 1) + n + 1

        def t_value(b, l, n):
            return b * 2 * (NU + 3) + l * (NU + 3) + n + 1

        def unit(b, l, k):
            return b * 2 * NU + l * NU + k

        def rq(g, t, h, n=1):
            at = (2 + 2 * g + t) * G + h
            return rms[:, at:at + n]

        def filled(eng, b, w):
            k, i = PLACE[w]
            eng.wait_ge(full[k], b * FILLS[k] + i + 1)

        def emptied(eng, b, w):
            k, i = PLACE[w]
            eng.wait_ge(free[k], b * FILLS[k] + i + 2)

        def emptied_all(eng, b, ws):
            last = {}
            for w in ws:
                last[PLACE[w][0]] = w
            for w in last.values():
                emptied(eng, b, w)

        def bank_of(w):
            return bank[PLACE[w][0]]

        def full_of(w):
            return full[PLACE[w][0]]

        def free_of(w):
            return free[PLACE[w][0]]

        @block.sync
        def _(sp):
            sp.dma_start(cst[:, :], consts).then_inc(in_cst, 16)
            sp.dma_start(spread_in, spread).then_inc(in_cst, 16)
            sp.dma_start(cin[:, :], ctxT[0]).then_inc(in_c, 16)
            sp.dma_start(xin[:, :, :], x[0].rearrange("(t p) d -> p t d", p=P)).then_inc(in_x, 16)
            sp.dma_start(w0x[:, 0:D], w0).then_inc(in_gat, 16)
            sp.dma_start(w1x[:, :, 0:D], w1.rearrange("(k p) n -> p k n", p=P)).then_inc(in_gat, 16)
            sp.dma_start(rows[:, :], gat_rows).then_inc(in_gat, 16)
            sp.dma_start(cols[:, :], norm_cols).then_inc(in_gat, 16)
            sp.dma_start(qkw[:, :], qk_rows).then_inc(in_gat, 16)
            sp.dma_start(wqkv_sb[:, :, :], wqkv.rearrange("(k p) n -> p k n", p=P)).then_inc(in_qkv, 16)
            sp.dma_start(wo_sb[:, :, :], wo.rearrange("(h p) n -> p h n", p=P)).then_inc(in_o, 16)
            sp.dma_start(wgate_sb[:, :, :], wgate.rearrange("(k p) n -> p k n", p=P)).then_inc(in_gu, 16)
            for m in range(2):
                sp.dma_start(wgu_sb[:, m, :, :], wgu[m].rearrange("(k p) n -> p k n", p=P)).then_inc(in_gu, 16)
            sp.dma_start(wd_sb[:, :, :], wd.rearrange("(j p) n -> p j n", p=P)).then_inc(in_d, 16)

            def load_inputs(b):
                sp.wait_ge(c_used, b)
                sp.dma_start(cin[:, :], ctxT[bass.ds(b, 1)].squeeze(0) if not isinstance(b, int) else ctxT[b]).then_inc(in_c, 16)
                sp.wait_ge(x_used, b)
                src = x[bass.ds(b, 1)].squeeze(0) if not isinstance(b, int) else x[b]
                sp.dma_start(xin[:, :, :], src.rearrange("(t p) d -> p t d", p=P)).then_inc(in_x, 16)

            def store(b):
                dst = out[bass.ds(b, 1)].squeeze(0) if not isinstance(b, int) else out[b]
                for t in range(T):
                    sp.wait_ge(y_ready, b * T + t + 1)
                    sp.dma_start(dst[t * P:(t + 1) * P, :], yo[:, t, :]).then_inc(out_free, 16)

            load_inputs(1)
            with sp.Fori(0, B - 2) as b:
                load_inputs(b + 2)
                store(b)
            store(B - 2)
            store(B - 1)
            sp.wait_ge(out_free, 16 * T * (B + 1))

        @block.tensor
        def _(pe):
            def gat(b, a):
                for l in range(2):
                    base = GAT[l]
                    if a == base:
                        if l == 0:
                            pe.wait_ge(in_c, (b + 1) * 16)
                            operands = [(cin, w0x)]
                        else:
                            pe.wait_ge(t_free, t_value(b, 0, NU + 2) + 1)
                            pe.nop(nofuse=True)
                            operands = [(gT[:, k, :], w1x[:, k, :]) for k in range(KT)]
                        pe.wait_ge(t_free, t_value(b, l, 0))
                        for t in range(T):
                            for i, (xt, w) in enumerate(operands):
                                mm = pe.matmul(tb[:, t * 2 * H:(t + 1) * 2 * H], xt[:, t * P:(t + 1) * P], w[:, D:D + 2 * H],
                                               start=(i == 0), stop=(i == len(operands) - 1))
                        mm.then_inc(t_full, 1)
                        pe.wait_ge(z_free, z_value(b, l, 0))
                        for t in range(T):
                            for i, (xt, w) in enumerate(operands):
                                mm = pe.matmul(zb[:, t * D:(t + 1) * D], xt[:, t * P:(t + 1) * P], w[:, 0:D],
                                               start=(i == 0), stop=(i == len(operands) - 1))
                        mm.then_inc(z_full, 1)
                    if a == base + 2:
                        pe.wait_ge(parts_ready, b * 2 + l + 1)
                        pe.wait_ge(t_free, t_value(b, l, 1))
                        pe.nop(nofuse=True)
                        for t in range(T):
                            mm = pe.transpose(tb[0:KZ, t * P // 2:(t + 1) * P // 2].bitcast(BF16),
                                              parts[:, t, :, :].rearrange("p a c -> p (a c)"), identb[:, :])
                        mm.then_inc(t_full, 1)
                    k = a - base - Z_AT
                    if 0 <= k < NU:
                        t, hp = divmod(k, H // 2)
                        if k == 0:
                            pe.wait_ge(pair_l_ready, b * 2 + l + 1)
                        if k in (0, 2):
                            pe.wait_ge(pair_r_ready, b * 4 + l * 2 + k // 2 + 1)
                        pe.wait_ge(z_free, z_value(b, l, k + 1))
                        pe.matmul(zb[:, :], pair_l[:, t * P:(t + 1) * P],
                                  pair_r[:, 2 * hp:2 * hp + 2, :].rearrange("k h m -> k (h m)"), start=True, stop=True)\
                          .then_inc(z_full, 1)
                    k = a - base - TURN_AT
                    if 0 <= k < NU:
                        pe.wait_ge(shifted, unit(b, l, k) + 1)
                        pe.wait_ge(t_free, t_value(b, l, k + 2))
                        for h in range(2):
                            for m in range(T):
                                mm = pe.transpose(tb[:, (h * T + m) * P:(h * T + m + 1) * P],
                                                  tt[:, k % 3, h, m * P:(m + 1) * P], ident)
                        mm.then_inc(t_full, 1)
                    k = a - base - PV_AT
                    if 0 <= k < NU:
                        t, hp = divmod(k, H // 2)
                        pe.wait_ge(t_free, t_value(b, l, k + 2) + 1)
                        if hp == 0:
                            pe.wait_ge(o_free, b * 2 * T + l * T + t + 1)
                        for h in range(2):
                            hh = 2 * hp + h
                            for m in range(T):
                                mm = pe.matmul(ob[:, hh * FE:(hh + 1) * FE], gpT[:, k % 2, h, m, :], feat[:, m, hh, :],
                                               start=(m == 0), stop=(m == T - 1))
                        mm.then_inc(pv_done, 1)
                if a in (GAT[0] + OUT_AT, HN_AT):
                    l = 0 if a != HN_AT else 1
                    if l == 0:
                        pe.wait_ge(gres_ready, (b + 1) * T)
                    else:
                        pe.wait_ge(hn_ready, b + 1)
                    pe.wait_ge(t_free, t_value(b, l, NU + 2))
                    for k in range(KT):
                        for t in range(T):
                            mm = pe.transpose(tb[:, (k * T + t) * P:(k * T + t + 1) * P], gex[:, t, k * P:(k + 1) * P], ident)
                    mm.then_inc(t_full, 1)

            def fill(b, w):
                kind, n = w
                ps = bank_of(w)
                bk, turn = PLACE[w]
                if kind == "qkv" and n == 0:
                    pe.wait_ge(t_free, t_value(b, 1, NU + 2) + 1)
                if kind == "turn":
                    if n < T:
                        pe.wait_ge(k_ready, (b + 1) * T)
                    else:
                        pe.wait_ge(m1_ready, b * QU + n + 4)
                        pe.wait_ge(m2_ready, b * QU + n + 4)
                if kind == "score":
                    g, j = divmod(n, 3)
                    t = min(j, 1)
                    emptied_all(pe, b, [("turn", t), ("turn", 2 + 2 * g + t)])
                if kind == "probT":
                    pe.wait_ge(prob_ready, b * 3 * HKV + n + 1)
                if kind == "av":
                    g, t = divmod(n, 2)
                    emptied_all(pe, b, [("probT", 3 * g + j) for j in ([0] if t == 0 else [1, 2])])
                if kind == "oproj":
                    emptied_all(pe, b, [("av", 2 * g + n) for g in range(HKV)])
                if kind == "h2T":
                    pe.wait_ge(h2n_ready, b * T + n + 1)
                if kind == "gate":
                    emptied_all(pe, b, [("h2T", t) for t in range(T)])
                if kind == "mixT":
                    pe.wait_ge(mix_ready, b + 1)
                if kind == "mix":
                    emptied_all(pe, b, [("mixT", t) for t in range(T)])
                if kind == "down":
                    emptied_all(pe, b, [("mix", p) for p in range(3)])
                if kind in ("score", "av", "oproj", "gate", "mix", "down"):
                    pe.nop(nofuse=True)
                pe.wait_ge(free[bk], b * FILLS[bk] + turn + 1)

                if kind == "qkv":
                    c, t = (HKV, n) if n < 2 else (HKV + 1, n - 2) if n < 4 else divmod(n - 4, 2)
                    for k in range(KT):
                        mm = pe.matmul(ps[:, :], hT[:, k, t * P:(t + 1) * P], wqkv_sb[:, k, c * G * HD:(c + 1) * G * HD],
                                       start=(k == 0), stop=(k == KT - 1))
                elif kind == "turn":
                    for h in range(G):
                        src, dst = (slice(h * HD, (h + 1) * HD)), ps[:, h * P:(h + 1) * P]
                        if n < T:
                            mm = pe.transpose(dst, m1[:, n % 4, src], ident)
                        else:
                            pe.matmul(dst, m1[:, n % 4, src], ident, is_transpose=True, start=True, stop=False)
                            mm = pe.matmul(dst, m2[:, n % 4, src], ident, is_transpose=True, start=False, stop=True)
                elif kind == "score":
                    nk = P * (t + 1)
                    heads = range(G) if t == 0 else range(2 * (j - 1), 2 * (j - 1) + 2)
                    for i, h in enumerate(heads):
                        pe.matmul(ps[:, i * nk:(i + 1) * nk], qT[:, G * g + h, t * P:(t + 1) * P], kT[:, g, 0:nk],
                                  start=True, stop=False)
                        mm = pe.matmul(ps[:, (i + 1) * nk - P:(i + 1) * nk], identb[:, :], causal[:, :], start=False, stop=True)
                elif kind == "probT":
                    g, j = divmod(n, 3)
                    if j == 0:
                        for h in range(G):
                            mm = pe.transpose(ps[:, h * P:(h + 1) * P], prob[:, n % 6, h * P:(h + 1) * P], ident)
                    else:
                        for m in range(T):
                            for h in range(2):
                                mm = pe.transpose(ps[:, (m * 2 + h) * P:(m * 2 + h + 1) * P],
                                                  prob[:, n % 6, h * N + m * P:h * N + (m + 1) * P], ident)
                elif kind == "av":
                    if t == 0:
                        mm = pe.matmul(ps[:, :], v_sb[:, 0, g * HD:(g + 1) * HD], pT0[:, :, :].rearrange("p h q -> p (h q)"),
                                       start=True, stop=True)
                    else:
                        for m in range(T):
                            mm = pe.matmul(ps[:, :], v_sb[:, m, g * HD:(g + 1) * HD],
                                           pT1[:, m, :, :].rearrange("p h q -> p (h q)"), start=(m == 0), stop=(m == T - 1))
                elif kind == "h2T":
                    for k in range(KT):
                        mm = pe.transpose(ps[:, k * P:(k + 1) * P], h2n[:, n, k * P:(k + 1) * P], ident)
                elif kind == "gate":
                    for t in range(T):
                        for k in range(KT):
                            mm = pe.matmul(ps[:, t * E:(t + 1) * E], tokT[:, k, t * P:(t + 1) * P], wgate_sb[:, k, :],
                                           start=(k == 0), stop=(k == KT - 1))
                elif kind == "updown":
                    for m in range(2):
                        for k in range(KT):
                            mm = pe.matmul(ps[:, m * N:(m + 1) * N], wgu_sb[:, m, k, n * P:(n + 1) * P], tokT[:, k, :],
                                           start=(k == 0), stop=(k == KT - 1))
                elif kind == "mixT":
                    mm = pe.transpose(ps[0:NP * E, 0:P // 2].bitcast(BF16), mixp[:, n, :, :].rearrange("p a e -> p (a e)"), identb[:, :])
                elif kind == "mix":
                    for i, j in enumerate(range(2 * n, min(2 * n + 2, JT))):
                        mm = pe.matmul(ps[:, i * N:(i + 1) * N], expert_rows[:, j * P:(j + 1) * P], mixT[:, :], start=True, stop=True)
                if kind not in ("oproj", "down"):
                    mm.then_inc(full[bk], 1)

            def long_products(b, s):
                if OPROJ <= s < OPROJ + T * O_PARTS:
                    t, part = divmod(s - OPROJ, O_PARTS)
                    w, k0, k1, last = ("oproj", t), part * HQ // O_PARTS, (part + 1) * HQ // O_PARTS, HQ - 1
                    lhs, rhs = oT, wo_sb
                elif DOWN <= s < DOWN + T * D_PARTS:
                    t, part = divmod(s - DOWN, D_PARTS)
                    w, (k0, k1), last = ("down", t), ((0, 6), (6, JT))[part], JT - 1
                    lhs, rhs = ah, wd_sb
                    if t == 0 and part == 1:
                        emptied_all(pe, b, [("mix", p) for p in range(3, (JT + 1) // 2)])
                else:
                    return
                for k in range(k0, k1):
                    mm = pe.matmul(bank_of(w)[:, 0:D], lhs[:, k, t * P:(t + 1) * P], rhs[:, k, :], start=(k == 0), stop=(k == last))
                if k1 == last + 1:
                    mm.then_inc(full_of(w), 1)

            pe.wait_ge(in_cst, 32)
            pe.wait_ge(setup_done, 1)
            for s in range(STEPS):
                gat(0, s)
            pe.wait_ge(in_qkv, 16)
            pe.wait_ge(in_o, 16)
            pe.wait_ge(in_gu, 48)
            pe.wait_ge(in_d, 16)
            with pe.Fori(0, B - 1) as b:
                for s in range(STEPS):
                    for w in work(s):
                        fill(b, w)
                    long_products(b, s)
                    gat(b + 1, s)
            for s in range(STEPS):
                for w in work(s):
                    fill(B - 1, w)
                long_products(B - 1, s)

        @block.scalar
        def _(act):
            def gat(b, a):
                for l in range(2):
                    base = GAT[l]
                    if a == base:
                        act.wait_ge(z_full, z_value(b, l, 0))
                        act.activation(feat[:, :, :, 0:FO], zb[:, :].rearrange("p (t h o) -> p t h o", t=T, h=H), ACT.Copy)\
                           .then_inc(z_free, 1)
                    if a in (base + 3, base + 4):
                        act.wait_ge(pair_l_ready, b * 2 + l + 1)
                        h0 = (a - base - 3) * H // 2
                        for h in range(h0, h0 + H // 2):
                            ins = act.activation(pair_r[:, h, :], partsT[:, :], ACT.Identity, bias=cst[0:KZ, C_ONE + h:C_ONE + h + 1],
                                                 scale=cst[0:KZ, C_PICK + h:C_PICK + h + 1])
                        ins.then_inc(pair_r_ready, 1)
                    k = a - base - Z_AT
                    if 0 <= k < NU:
                        act.wait_ge(z_full, z_value(b, l, k + 1))
                        act.wait_ge(lrelu_done, unit(b, l, k) + 1)
                        act.activation(zs[:, k % 2, :], zb[:, :], ACT.Copy, scale=-1.0).then_inc(z_free, 1)
                    k = a - base - TURN_AT
                    if 0 <= k < NU:
                        act.wait_ge(t_full, t_value(b, l, k + 2))
                        if k >= 2:
                            act.wait_ge(pv_done, unit(b, l, k) - 1)
                        act.activation(gpT[:, k % 2, :, :, :].rearrange("p h m i -> p (h m i)"), tb[:, :], ACT.Exp).then_inc(t_free, 1)
                    for t in range(T):
                        if a == base + PV_AT + 4 * t + 4:
                            act.wait_ge(gout_ready, b * 2 * T + l * T + t + 1)
                            act.activation(gex[:, t, :], go[:, t, :], ACT.Exp).then_inc(gexp_ready, 1)

            def empty(b, w):
                kind, n = w
                ps = bank_of(w)
                if kind == "qkv":
                    filled(act, b, w)
                    if n in (2, 3):
                        act.activation(v_sb[:, n - 2, :], ps[:, :], ACT.Copy).then_inc(free_of(w), 1)
                    else:
                        u = n if n < 2 else n - 2
                        act.wait_ge(m1_ready, b * QU + u + 1)
                        act.wait_ge(m2_ready, b * QU + u + 1)
                        act.activation(raw[:, u % 3, :], ps[:, :], ACT.Copy).then_inc(raw_ready, 1)
                        act.activation(sq[:, u % 3, :], ps[:, :], ACT.Square).then_inc(free_of(w), 1)
                elif kind == "turn":
                    filled(act, b, w)
                    if n < 2:
                        dst = kT[:, :, n * P:(n + 1) * P]
                    else:
                        g, t = divmod(n - 2, 2)
                        dst = qT[:, G * g:G * g + G, t * P:(t + 1) * P]
                    act.activation(dst, ps[:, :].rearrange("p (h q) -> p h q", h=G), ACT.Copy).then_inc(free_of(w), 1)
                elif kind == "score":
                    g, j = divmod(n, 3)
                    t = min(j, 1)
                    nk = P * (t + 1)
                    heads = range(G) if t == 0 else range(2 * (j - 1), 2 * (j - 1) + 2)
                    act.wait_ge(sneg_ready, b * 3 * HKV + n + 1)
                    if n >= 6:
                        filled(act, b, ("probT", n - 6))
                    for i, h in enumerate(heads):
                        ins = act.activation(prob[:, n % 6, i * nk:(i + 1) * nk], ps[:, i * nk:(i + 1) * nk], ACT.Exp,
                                             bias=sneg[:, n, i:i + 1], scale=rq(g, t, h), accum_out=ssum[:, n, i:i + 1])
                    ins.then_inc(free_of(w), 1)
                elif kind == "av":
                    g, t = divmod(n, 2)
                    filled(act, b, w)
                    act.activation(oT[:, G * g:G * g + G, t * P:(t + 1) * P], ps[:, :].rearrange("p (h q) -> p h q", h=G), ACT.Copy)\
                       .then_inc(free_of(w), 1)
                elif kind == "gate":
                    for t in range(T):
                        act.wait_ge(lneg_ready, b * T + t + 1)
                        act.activation(lex[:, t, :], lg[:, t, :], ACT.Exp, bias=lmx[:, t:t + 1]).then_inc(lexp_ready, 1)
                elif kind == "updown":
                    filled(act, b, w)
                    if n >= 3:
                        emptied(act, b, ("updown", n - 3))
                    act.activation(th[:, n % 3, :], ps[:, 0:N], ACT.Tanh, scale=0.5).then_inc(tanh_ready, 1)

            for s in range(STEPS):
                gat(0, s)
            with act.Fori(0, B - 1) as b:
                for s in range(STEPS):
                    for w in use(s):
                        empty(b, w)
                    gat(b + 1, s)
            for s in range(STEPS):
                for w in use(s):
                    empty(B - 1, w)

        @block.gpsimd
        def _(pool):
            def gat(b, a):
                for l in range(2):
                    k = a - GAT[l] - TTR_AT
                    if 0 <= k < NU:
                        pool.wait_ge(score_ready, unit(b, l, k) + 1)
                        pool.nop(nofuse=True)
                        for h in range(2):
                            ins = pool.tensor_scalar(tt[:, k % 3, h, :], tt[:, k % 3, h, :], -1.0, gmn[:, k % 3, h:h + 1],
                                                     ALU.mult, ALU.add)
                        ins.then_inc(shifted, 1)

            links = [0]

            def link(b, ins):
                links[0] += 1
                ins.then_inc(pool_b, 1)
                pool.wait_ge(pool_b, b * N_P + links[0])

            def inverse_rms(b, c):
                lo, hi = ((0, 2 * G), (2 * G, 6 * G), (6 * G, 10 * G))[c]
                v, y, a = ssq[:, lo:hi], rms[:, lo:hi], rms_a[:, lo:hi]
                pool.wait_ge(seed_ready, b * 3 + c + 1)
                for _ in range(3):
                    link(b, pool.tensor_tensor(a, y, y, ALU.mult))
                    link(b, pool.tensor_tensor(a, a, v, ALU.mult))
                    pool.nop(nofuse=True)
                    link(b, pool.tensor_scalar(a, a, -0.5, 1.5, ALU.mult, ALU.add))
                    if _ < 2 or c:
                        link(b, pool.tensor_tensor(y, y, a, ALU.mult))
                    else:
                        pool.tensor_tensor(y, y, a, ALU.mult).then_inc(rms_ready, 1)
                if c:
                    pool.nop(nofuse=True)
                    pool.tensor_scalar(y, y, SCALE, 1.0, ALU.mult, ALU.mult).then_inc(rms_ready, 1)

            def part(b, w):
                kind, n = w
                if kind == "qkv" and n not in (2, 3):
                    u = n if n < 2 else n - 2
                    which, t = (1, u) if u < 2 else (0, u % 2)
                    pool.wait_ge(raw_ready, b * QU + u + 1)
                    if u >= 4:
                        filled(pool, b, ("turn", u - 4))
                    src = raw[:, u % 3, :].rearrange("p (h c d) -> p h c d", h=G, c=2)
                    dst = m2[:, u % 4, :].rearrange("p (h c d) -> p h c d", h=G, c=2)
                    for c in range(2):
                        s_ = rope_s[:, which, t, c * HD // 2:(c + 1) * HD // 2].unsqueeze(1).broadcast_to([P, G, HD // 2])
                        ins = pool.tensor_tensor(dst[:, :, c, :], src[:, :, 1 - c, :], s_, ALU.mult)
                    ins.then_inc(m2_ready, 1)
                    if u in (1, 5, 9):
                        inverse_rms(b, (u - 1) // 4)
                elif kind == "oproj":
                    pool.wait_ge(hid2_ready, b * T + n + 1)
                    pool.tensor_tensor(osum[:, n, :], x1[:, n, :], hid2[:, n, :], ALU.add).then_inc(osum_ready, 1)

            def normalise(b, s):
                for n in summed(s):
                    nh, nk = (G, P) if n % 3 == 0 else (2, N)
                    pool.wait_ge(srcp_ready, b * 3 * HKV + n + 1)
                    pool.nop(nofuse=True)
                    for i in range(nh):
                        part_ = prob[:, n % 6, i * nk:(i + 1) * nk]
                        ins = pool.tensor_scalar(part_, part_, srcp[:, n, i:i + 1], 1.0, ALU.mult, ALU.mult)
                    ins.then_inc(prob_ready, 1)

            pool.wait_ge(setup_done, 1)
            for s in range(STEPS):
                gat(0, s)
            with pool.Fori(0, B - 1) as b:
                links[0] = 0
                for s in range(STEPS):
                    for w in use(s):
                        part(b, w)
                    normalise(b, s)
                    gat(b + 1, s)
            assert links[0] == N_P, links
            links[0] = 0
            for s in range(STEPS):
                for w in use(s):
                    part(B - 1, w)
                normalise(B - 1, s)

        A_LINKS, B_LINKS = [0], [0]

        @block.vector
        def _(dve):
            count = [0, 0]

            def link_a(b, ins):
                count[0] += 1
                ins.then_inc(dve_a, 1)
                dve.wait_ge(dve_a, b * N_A + count[0])

            def link_b(b, ins):
                count[1] += 1
                ins.then_inc(dve_b, 1)
                dve.wait_ge(dve_b, b * N_B + count[1])

            def rsqrt(link, b, y, a, v):
                link(b, dve.tensor_scalar(a.bitcast(I32), v.bitcast(I32), 1, None, ALU.logical_shift_right))
                link(b, dve.tensor_scalar(y.bitcast(I32), a.bitcast(I32), -1, MAGIC, ALU.mult, ALU.add))
                for _ in range(3):
                    link(b, dve.scalar_tensor_tensor(a, y, -0.5, y, ALU.mult, ALU.mult))
                    link(b, dve.tensor_tensor(a, a, v, ALU.mult))
                    link(b, dve.scalar_tensor_tensor(y, a, 1.5, y, ALU.add, ALU.mult))

            def moments(b, src):
                for t in range(T):
                    ins = dve.bn_stats(stats[:, t, :], src[:, t, :])
                link_a(b, ins)
                dve.nop(nofuse=True)
                for t in range(T):
                    ins = dve.bn_aggr(mv[:, t, :], stats[:, t, :])
                link_a(b, ins)

            def gat(b, a):
                if a == 0:
                    dve.wait_ge(in_x, (b + 1) * 16)
                    moments(b, xin)
                    link_a(b, dve.tensor_scalar(rs_v[:, 0:T], mv[:, :, 1], LN_EPS, None, ALU.add))
                    rsqrt(link_a, b, rs_y[:, 0:T], rs_a[:, 0:T], rs_v[:, 0:T])
                    for t in range(T):
                        ins = dve.tensor_scalar(maskv[:, t, :], xin[:, t, :], mv[:, t, 0:1], rs_y[:, t:t + 1], ALU.subtract, ALU.mult)
                    link_a(b, ins)
                    link_a(b, dve.tensor_scalar(maskv[:, :, :], maskv[:, :, :], 1.0, -1e10, ALU.subtract, ALU.mult))
                for l in range(2):
                    base = GAT[l]
                    if a == base:
                        dve.wait_ge(t_full, t_value(b, l, 0))
                        ps = tb[:, 0:T * 2 * H].rearrange("p (t c) -> p t c", t=T)
                        link_a(b, dve.tensor_copy(parts[:, :, 0, :], ps))
                        dve.tensor_tensor(sn_res[:, :, :], ps, parts[:, :, 0, :], ALU.subtract).then_inc(t_free, 1)
                        dve.wait_ge(t_free, t_value(b, l, 0) + 1)
                        link_a(b, dve.tensor_copy(parts[:, :, 1, :], sn_res[:, :, :]))
                        dve.tensor_tensor(parts[:, :, 2, :], sn_res[:, :, :], parts[:, :, 1, :], ALU.subtract).then_inc(parts_ready, 1)
                        if l == 0:
                            dve.wait_ge(z_full, z_value(b, 0, 0))
                            dve.sem_inc(c_used, 1)
                    if a == base + 2:
                        dve.wait_ge(t_full, t_value(b, l, 1))
                        dve.tensor_copy(partsT[:, :], tb[0:KZ, 0:N // 2].bitcast(BF16)).then_inc(t_free, 1)
                        dve.wait_ge(t_free, t_value(b, l, 1) + 1)
                        dve.tensor_scalar(pair_l[:, :], partsT[:, :], cst[0:KZ, C_SELF:C_SELF + 1], cst[0:KZ, C_NEIGH:C_NEIGH + 1],
                                          ALU.mult, ALU.add).then_inc(pair_l_ready, 1)
                    k = a - base - Z_AT
                    if 0 <= k < NU:
                        dve.wait_ge(z_free, z_value(b, l, k + 1) + 1)
                        if k >= 2:
                            dve.wait_ge(score_ready, unit(b, l, k) - 1)
                        dve.scalar_tensor_tensor(lr[:, k % 2, :], zs[:, k % 2, :], 0.2, zs[:, k % 2, :], ALU.mult, ALU.min)\
                           .then_inc(lrelu_done, 1)
                    k = a - base - TTR_AT
                    if 0 <= k < NU:
                        t, hp = divmod(k, H // 2)
                        dve.wait_ge(lrelu_done, unit(b, l, k) + 3)
                        if k >= 3:
                            dve.wait_ge(t_full, t_value(b, l, k - 1))
                        dve.nop(nofuse=True)
                        for h in range(2):
                            ins = dve.tensor_tensor_reduce(tt[:, k % 3, h, :], lr[:, k % 2, h * N:(h + 1) * N], maskv[:, t, :], 1.0, 3e38,
                                                           ALU.add, ALU.min, gmn[:, k % 3, h:h + 1])
                        ins.then_inc(score_ready, 1)
                    for t in range(T):
                        if a == base + PV_AT + 4 * t + 3:
                            dve.wait_ge(pv_done, unit(b, l, 4 * t + 4))
                            o_ = ob[:, 0:H * FE].rearrange("p (h o) -> p h o", h=H)
                            link_a(b, dve.reciprocal(gsum[:, :], o_[:, :, FO]))
                            g_ = go[:, t, :].rearrange("p (h o) -> p h o", h=H)
                            dve.tensor_tensor(g_, o_[:, :, 0:FO], gsum[:, :].unsqueeze(2).broadcast_to([P, H, FO]), ALU.mult)\
                               .then_inc(o_free, 1)
                            dve.wait_ge(o_free, b * 2 * T + l * T + t + 2)
                            dve.tensor_tensor(go[:, t, :], go[:, t, :], rows[:, (3 * l + 2) * D:(3 * l + 3) * D], ALU.add)\
                               .then_inc(gout_ready, 1)
                        if a == base + PV_AT + 4 * t + 4:
                            dve.wait_ge(gexp_ready, b * 2 * T + l * T + t + 1)
                            link_a(b, dve.tensor_scalar(gex[:, t, :], gex[:, t, :], 1.0, -1.0, ALU.min, ALU.add))
                            ins = dve.scalar_tensor_tensor(gex[:, t, :], go[:, t, :], 0.0, gex[:, t, :], ALU.max, ALU.add)
                            if l == 0:
                                ins.then_inc(gres_ready, 1)
                            else:
                                link_a(b, ins)
                                link_a(b, dve.tensor_tensor(x1[:, t, :], xin[:, t, :], gex[:, t, :], ALU.add))
                                if t == T - 1:
                                    dve.sem_inc(x_used, 1)
                if a == GAT[0] + OUT_AT:
                    dve.wait_ge(t_full, t_value(b, 0, NU + 2))
                    dve.tensor_copy(gT[:, :, :].rearrange("p k n -> p (k n)"), tb[:, :]).then_inc(t_free, 1)
                if a == LN2_AT:
                    moments(b, x1)
                    link_a(b, dve.tensor_scalar(rs_v[:, 0:T], mv[:, :, 1], LN_EPS, None, ALU.add))
                    link_a(b, dve.scalar_tensor_tensor(rs_v[:, T:2 * T], rs_v[:, 0:T], RMS_EPS, mv[:, :, 1], ALU.mult, ALU.add))
                    rsqrt(link_a, b, rs_y[:, :], rs_a[:, :], rs_v[:, :])
                    for t in range(T):
                        ins = dve.tensor_scalar(hn[:, t, :], x1[:, t, :], mv[:, t, 0:1], rs_y[:, T + t:T + t + 1], ALU.subtract, ALU.mult)
                    ins.then_inc(hn_ready, 1)
                    for t in range(T):
                        ins = dve.tensor_scalar(hid[:, t, :], x1[:, t, :], mv[:, t, 0:1], rs_y[:, t:t + 1], ALU.subtract, ALU.mult)
                    link_a(b, ins)
                if a == HN_AT:
                    dve.wait_ge(t_full, t_value(b, 1, NU + 2))
                    for k in range(KT):
                        ins = dve.tensor_scalar(hT[:, k, :], tb[:, k * N:(k + 1) * N], cols[:, k:k + 1], None, ALU.mult)
                    ins.then_inc(t_free, 1)

            def part(b, w):
                kind, n = w
                ps = bank_of(w)
                if kind == "qkv" and n not in (2, 3):
                    u = n if n < 2 else n - 2
                    which, t = (1, u) if u < 2 else (0, u % 2)
                    dve.wait_ge(raw_ready, b * QU + u + 1)
                    if u >= 4:
                        filled(dve, b, ("turn", u - 4))
                    c_ = rope_c[:, which, t, :].unsqueeze(1).broadcast_to([P, G, HD])
                    ins = dve.tensor_tensor(m1[:, u % 4, :].rearrange("p (h d) -> p h d", h=G),
                                            raw[:, u % 3, :].rearrange("p (h d) -> p h d", h=G), c_, ALU.mult)
                    emptied(dve, b, w)
                    ins = dve.tensor_reduce(ssq[:, u * G:(u + 1) * G], sq[:, u % 3, :].rearrange("p (h d) -> p h d", h=G), AX.X, ALU.add)
                    ins.then_inc(m1_ready, 1)
                    if u in (1, 5, 9):
                        lo, hi = ((0, 2 * G), (2 * G, 6 * G), (6 * G, 10 * G))[(u - 1) // 4]
                        v, y, a = ssq[:, lo:hi], rms[:, lo:hi], rms_a[:, lo:hi]
                        dve.wait_ge(m1_ready, b * QU + u + 4)
                        link_b(b, dve.tensor_scalar(v, v, 1.0 / HD, RMS_EPS, ALU.mult, ALU.add))
                        link_b(b, dve.tensor_scalar(a.bitcast(I32), v.bitcast(I32), 1, None, ALU.logical_shift_right))
                        dve.tensor_scalar(y.bitcast(I32), a.bitcast(I32), -1, MAGIC, ALU.mult, ALU.add).then_inc(seed_ready, 1)
                elif kind == "qkv" and n == 3:
                    dve.wait_ge(m2_ready, b * QU + 5)
                    dve.wait_ge(m1_ready, b * QU + 5)
                    for u in range(T):
                        ins = dve.tensor_tensor(m1[:, u, :], m1[:, u, :], m2[:, u, :], ALU.add)
                    link_b(b, ins)
                    dve.wait_ge(rms_ready, b * 3 + 1)
                    for u in range(T):
                        r_ = m1[:, u, :].rearrange("p (h d) -> p h d", h=G)
                        dve.tensor_tensor(r_, r_, rms[:, u * G:(u + 1) * G].unsqueeze(2).broadcast_to([P, G, HD]), ALU.mult)\
                           .then_inc(k_ready, 1)
                elif kind == "score":
                    g, j = divmod(n, 3)
                    t = min(j, 1)
                    nh, nk = (G, P) if j == 0 else (2, N)
                    h0 = 0 if j == 0 else 2 * (j - 1)
                    if n in (0, 6):
                        dve.wait_ge(rms_ready, b * 3 + 2 + n // 6)
                    filled(dve, b, w)
                    link_b(b, dve.tensor_reduce(smx[:, n, 0:nh], ps[:, :].rearrange("p (h k) -> p h k", h=nh), AX.X, ALU.max))
                    dve.scalar_tensor_tensor(sneg[:, n, 0:nh], smx[:, n, 0:nh], -1.0, rq(g, t, h0, nh), ALU.mult, ALU.mult)\
                       .then_inc(sneg_ready, 1)
                elif kind == "probT":
                    g, j = divmod(n, 3)
                    filled(dve, b, w)
                    if j == 0:
                        if g:
                            filled(dve, b, ("av", 2 * (g - 1)))
                        dve.tensor_copy(pT0[:, :, :].rearrange("p h q -> p (h q)"), ps[:, :]).then_inc(free_of(w), 1)
                    else:
                        if g:
                            filled(dve, b, ("av", 2 * (g - 1) + 1))
                        dve.tensor_copy(pT1[:, :, 2 * (j - 1):2 * j, :], ps[:, :].rearrange("p (m h q) -> p m h q", m=T, h=2))\
                           .then_inc(free_of(w), 1)
                elif kind == "oproj":
                    filled(dve, b, w)
                    dve.tensor_tensor(hid2[:, n, :], ps[:, 0:D], hid[:, n, :], ALU.add).then_inc(free_of(w), 1)
                    emptied(dve, b, w)
                    dve.tensor_tensor_reduce(h2n[:, n, :], hid2[:, n, :], hid2[:, n, :], 1.0, 0.0, ALU.mult, ALU.add, ss2[:, n:n + 1])\
                       .then_inc(hid2_ready, 1)
                    dve.wait_ge(hid2_ready, b * T + n + 1)
                    one = slice(n, n + 1)
                    link_b(b, dve.tensor_scalar(h2_v[:, one], ss2[:, one], 1.0 / D, RMS_EPS, ALU.mult, ALU.add))
                    rsqrt(link_b, b, h2_y[:, one], h2_a[:, one], h2_v[:, one])
                    dve.tensor_scalar(h2n[:, n, :], hid2[:, n, :], h2_y[:, one], None, ALU.mult).then_inc(h2n_ready, 1)
                elif kind == "h2T":
                    filled(dve, b, w)
                    for k in range(KT):
                        ins = dve.tensor_scalar(tokT[:, k, n * P:(n + 1) * P], ps[:, k * P:(k + 1) * P], cols[:, KT + k:KT + k + 1], None,
                                                ALU.mult)
                    ins.then_inc(free_of(w), 1)
                elif kind == "gate":
                    filled(dve, b, w)
                    link_b(b, dve.tensor_copy(lg[:, :, :].rearrange("p t e -> p (t e)"), ps[:, 0:T * E]))
                    ins = dve.tensor_reduce(lmx[:, :], lg[:, :, :], AX.X, ALU.max)
                    ins.then_inc(free_of(w), 1)
                    emptied(dve, b, w)
                    for t in range(T):
                        dve.tensor_scalar(lmx[:, t:t + 1], lmx[:, t:t + 1], -1.0, None, ALU.mult).then_inc(lneg_ready, 1)
                elif kind == "updown":
                    if n == 0:
                        dve.wait_ge(osum_ready, (b + 1) * T)
                    if n == 1:
                        mixing(b)
                    dve.wait_ge(tanh_ready, b * JT + n + 1)
                    link_b(b, dve.scalar_tensor_tensor(ga[:, :], th[:, n % 3, :], 1.0, ps[:, 0:N], ALU.add, ALU.mult))
                    dve.scalar_tensor_tensor(ah[:, n, :], ga[:, :], 0.5, ps[:, N:2 * N], ALU.mult, ALU.mult).then_inc(free_of(w), 1)
                    emptied(dve, b, w)
                elif kind == "mixT":
                    filled(dve, b, w)
                    dve.tensor_copy(mixT[:, n * P:(n + 1) * P], ps[0:NP * E, 0:P // 2].bitcast(BF16)).then_inc(free_of(w), 1)
                elif kind == "mix":
                    filled(dve, b, w)
                    j0, j1 = 2 * n, min(2 * n + 2, JT)
                    a_ = ah[:, j0:j1, :].rearrange("p j n -> p (j n)")
                    dve.tensor_tensor(a_, a_, ps[:, 0:(j1 - j0) * N], ALU.mult).then_inc(free_of(w), 1)
                elif kind == "down":
                    filled(dve, b, w)
                    dve.wait_ge(osum_ready, b * T + n + 1)
                    dve.wait_ge(out_free, (b + 1) * 16 * T)
                    dve.tensor_tensor(yo[:, n, :], osum[:, n, :], ps[:, 0:D], ALU.add).then_inc(free_of(w), 1)
                    emptied(dve, b, w)
                    dve.sem_inc(y_ready, 1)

            def reciprocals(b, s):
                for n in summed(s):
                    nh = G if n % 3 == 0 else 2
                    emptied(dve, b, ("score", n))
                    dve.reciprocal(srcp[:, n, 0:nh], ssum[:, n, 0:nh]).then_inc(srcp_ready, 1)

            def mixing(b):
                dve.wait_ge(lexp_ready, (b + 1) * T)
                link_b(b, dve.tensor_reduce(lmx[:, :], lex[:, :, :], AX.X, ALU.add))
                link_b(b, dve.reciprocal(lmx[:, :], lmx[:, :]))
                link_b(b, dve.tensor_tensor(lex[:, :, :], lex[:, :, :], lmx[:, :].unsqueeze(2).broadcast_to([P, T, E]), ALU.mult))
                tri = cst[:, C_TRI:C_TRI + E * E].rearrange("p (e j) -> p e j", e=E)
                for t in range(T):
                    mine = lex[:, t, :].unsqueeze(2).broadcast_to([P, E, E])
                    other = lex[:, t, :].unsqueeze(1).broadcast_to([P, E, E])
                    link_b(b, dve.tensor_tensor(cmp1[:, t, :, :], other, mine, ALU.is_gt))
                    link_b(b, dve.tensor_tensor(cmp2[:, t, :, :], other, mine, ALU.is_equal))
                    link_b(b, dve.tensor_tensor(cmp2[:, t, :, :], cmp2[:, t, :, :], tri, ALU.mult))
                    link_b(b, dve.tensor_tensor(cmp1[:, t, :, :], cmp1[:, t, :, :], cmp2[:, t, :, :], ALU.add))
                link_b(b, dve.tensor_reduce(rank[:, :, :], cmp1[:, :, :, :], AX.X, ALU.add))
                link_b(b, dve.scalar_tensor_tensor(lex[:, :, :], rank[:, :, :], 2.0, lex[:, :, :], ALU.is_lt, ALU.mult))
                link_b(b, dve.tensor_reduce(lmx[:, :], lex[:, :, :], AX.X, ALU.add))
                link_b(b, dve.tensor_scalar(lmx[:, :], lmx[:, :], 1e-9, None, ALU.add))
                link_b(b, dve.reciprocal(lmx[:, :], lmx[:, :]))
                link_b(b, dve.tensor_tensor(lex[:, :, :], lex[:, :, :], lmx[:, :].unsqueeze(2).broadcast_to([P, T, E]), ALU.mult))
                link_b(b, dve.tensor_copy(mixp[:, :, 0, :], lex[:, :, :]))
                link_b(b, dve.tensor_tensor(rank[:, :, :], lex[:, :, :], mixp[:, :, 0, :], ALU.subtract))
                link_b(b, dve.tensor_copy(mixp[:, :, 1, :], rank[:, :, :]))
                dve.tensor_tensor(mixp[:, :, 2, :], rank[:, :, :], mixp[:, :, 1, :], ALU.subtract).then_inc(mix_ready, 1)

            n_setup = [0]

            def link(ins):
                n_setup[0] += 1
                ins.then_inc(setup_v, 1)
                dve.wait_ge(setup_v, n_setup[0])

            dve.wait_ge(in_cst, 32)
            link(dve.tensor_copy(identb[:, :], ident))
            link(dve.tensor_copy(causal[:, :], cst[:, C_CAUSAL:C_CAUSAL + P]))
            link(dve.tensor_copy(expert_rows[:, :], spread_in))
            for t in range(T):
                link(dve.memset(feat[:, t, :, FO:FE], 1.0))
            dve.wait_ge(in_gat, 80)
            for l in range(2):
                for k in range(1 if l == 0 else KT):
                    wx = w0x[:, :] if l == 0 else w1x[:, k, :]
                    np_ = F_IN if l == 0 else P
                    for v in range(2):
                        link(dve.tensor_tensor(wprod[0:np_, :], wx[:, 0:D], rows[0:np_, (3 * l + v) * D:(3 * l + v + 1) * D], ALU.mult))
                        link(dve.tensor_reduce(wx[:, D + v * H:D + (v + 1) * H], wprod[0:np_, :].rearrange("p (h o) -> p h o", h=H),
                                               AX.X, ALU.add))
            for m in range(2):
                for t in range(T):
                    w_ = qkw[:, m * HD:(m + 1) * HD]
                    link(dve.tensor_tensor(rope_c[:, m, t, :], cst[:, C_COS + t * HD:C_COS + (t + 1) * HD], w_, ALU.mult))
                    for c in range(2):
                        half = slice(c * HD // 2, (c + 1) * HD // 2)
                        link(dve.tensor_tensor(rope_s[:, m, t, half], cst[:, C_SIN + t * HD + c * HD // 2:C_SIN + t * HD + (c + 1) * HD // 2],
                                               qkw[:, m * HD + (1 - c) * HD // 2:m * HD + (2 - c) * HD // 2], ALU.mult))
            dve.sem_inc(z_free, 1)
            dve.sem_inc(t_free, 1)
            dve.sem_inc(o_free, 1)
            dve.sem_inc(lrelu_done, 2)
            dve.sem_inc(m1_ready, 3)
            dve.sem_inc(m2_ready, 3)
            dve.sem_inc(out_free, 16 * T)
            for k in range(BANKS):
                dve.sem_inc(free[k], 1)
            dve.sem_inc(setup_done, 1)
            for s in range(STEPS):
                gat(0, s)
            assert count[0] == N_A, count
            with dve.Fori(0, B - 1) as b:
                count[:] = [0, 0]
                for s in range(STEPS):
                    for w in use(s):
                        part(b, w)
                    reciprocals(b, s)
                    gat(b + 1, s)
            assert count[1] == N_B, count
            count[:] = [0, 0]
            for s in range(STEPS):
                for w in use(s):
                    part(B - 1, w)
                reciprocals(B - 1, s)


def kernel(**inputs):
    import numpy as _np
    import concourse.bacc as _bacc
    from concourse import mybir as _mybir
    from concourse.bass_utils import run_bass_kernel_spmd as _run

    i = {k: _np.asarray(v) for k, v in inputs.items()}
    g = {k[len("L0_xattn_"):]: v for k, v in i.items() if k.startswith("L0_xattn_")}
    f = {k[len("L0_ffn_"):]: v for k, v in i.items() if k.startswith("L0_ffn_")}

    def on_rows(*vectors):
        return _np.concatenate([_np.broadcast_to(v.reshape(1, -1), (P, v.size)) for v in vectors], 1)

    arrays = {
        "x": i["x"],
        "ctxT": i["ctx_512"].transpose(0, 2, 1),
        "w0": g["W0"].transpose(1, 0, 2).reshape(F_IN, D),
        "w1": g["W1"].transpose(1, 0, 2).reshape(D, D),
        "gat_rows": on_rows(g["a_self0"], g["a_neigh0"], g["b0"], g["a_self1"], g["a_neigh1"], g["b1"]),
        "norm_cols": _np.concatenate([f["attn_norm_w"].reshape(KT, P).T, f["ffn_norm_w"].reshape(KT, P).T], 1),
        "qk_rows": on_rows(f["q_norm_w"], f["k_norm_w"]),
        "wqkv": _np.concatenate([f["q_w"], f["k_w"], f["v_w"]], 0).T,
        "wo": f["o_w"].T,
        "wgate": f["gate_w"].T,
        "wgu": _np.stack([f["wg"].reshape(EI, D).T, f["wu"].reshape(EI, D).T]),
        "wd": f["wd"].transpose(0, 2, 1).reshape(EI, D),
        "consts": constants()[0],
        "spread": constants()[1],
    }
    arrays = {k + "_dram": _np.ascontiguousarray(v) for k, v in arrays.items()}
    nc = _bacc.Bacc("TRN2", target_bir_lowering=False, num_devices=1)
    args = [nc.dram_tensor(k, v.shape, _mybir.dt.from_np(v.dtype), kind="ExternalInput").ap() for k, v in arrays.items()]
    args.append(nc.dram_tensor("out_dram", (B, N, D), _mybir.dt.float32, kind="ExternalOutput").ap())
    block_program(nc, *args)
    r = _run(nc, [arrays], core_ids=[0])
    return r.results[0]["out_dram"]
```

```python
import concourse.bass as bass
from concourse import mybir
from contextlib import ExitStack
import numpy as np

F32 = mybir.dt.float32
I32 = mybir.dt.int32
BF16 = mybir.dt.bfloat16
ALU = mybir.AluOpType
ACT = mybir.ActivationFunctionType
AX = mybir.AxisListType

P = 128
B, N, D = 4, 256, 256
T = N // P
KT = D // P
F_IN = 64
H, FO = 8, 32
FE = FO + 1
NP = 3
KZ = NP * 2 * H
HQ, HKV, HD = 16, 4, 128
G = HQ // HKV
E, I = 8, 176
EI = E * I
JT = EI // P
NU = 2 * T * 2
QU = (HQ + HKV) // G * T
LN_EPS, RMS_EPS = 1e-5, 1e-6
SCALE = float(HD) ** -0.5
MASKED = -1e30
MAGIC = 0x5F3759DF

C_ID = 0
C_CAUSAL = C_ID + P
C_COS = C_CAUSAL + P
C_SIN = C_COS + T * HD
C_PICK = C_SIN + T * HD
C_ONE = C_PICK + H
C_SELF = C_ONE + H
C_NEIGH = C_SELF + 1
C_TRI = C_NEIGH + 1
C_END = C_TRI + E * E


def constants():
    c = np.zeros((P, C_END), np.float32)
    c[:, C_ID:C_ID + P] = np.eye(P)
    c[:, C_CAUSAL:C_CAUSAL + P] = np.where(np.arange(P)[None, :] > np.arange(P)[:, None], MASKED, 0.0)
    freqs = (np.float32(1.0) / np.float32(1e6) ** (np.arange(0, HD, 2, dtype=np.float32) / np.float32(HD))).astype(np.float32)
    angle = np.outer(np.arange(N, dtype=np.float32), freqs).astype(np.float32)
    cos, sin = np.cos(angle), np.sin(angle)
    for t in range(T):
        rows = slice(t * P, (t + 1) * P)
        c[:, C_COS + t * HD:C_COS + (t + 1) * HD] = np.concatenate([cos[rows], cos[rows]], 1)
        c[:, C_SIN + t * HD:C_SIN + (t + 1) * HD] = np.concatenate([-sin[rows], sin[rows]], 1)
    for p in range(NP):
        for h in range(H):
            self_row, neigh_row = p * 2 * H + h, p * 2 * H + H + h
            c[neigh_row, C_PICK + h] = 1.0
            c[self_row, C_ONE + h] = 1.0
            c[self_row, C_SELF] = 1.0
            c[neigh_row, C_NEIGH] = 1.0
    for e in range(E):
        c[:, C_TRI + e * E:C_TRI + e * E + e] = 1.0
    spread = np.tile(np.repeat(np.eye(E, dtype=np.float32), I, axis=1), (NP, 1))
    return c, spread


N_A, N_B, N_P = 39, 64, 36

STEPS = 48
TERMS_AT = (1, 22)
PARTS_AT = (2, 24)
PAIRS_AT = (3, 26)
UNIT_AT = ((5, 6, 7, 8, 9, 10, 11, 12), (28, 29, 30, 31, 32, 33, 34, 35))
SCORE_LAG, TRANS_LAG, PV_LAG = 1, 4, 5
ELU_LAG = 1
MASK_AT = (2, 3, 4)
OUT_AT = 20
LN2_AT = (44, 44, 46)
HN_AT = 47
QKV_AT = (1, 2, 3, 4, 5, 6, 7, 8, 9, 10, 11, 11)
TURN_AT = (6, 7, 8, 9, 10, 11, 11, 12, 13, 14)
SCORE_AT = (10, 11, 12, 13, 14, 15, 16, 17, 18, 19, 20, 21)
SUM_AT = (12, 13, 14, 15, 15, 16, 17, 18, 19, 20, 21, 22)
PROBT_AT = (14, 15, 16, 17, 18, 19, 20, 21, 21, 22, 23, 24)
AV_AT = (15, 17, 18, 20, 21, 22, 23, 25)
OPROJ_AT = (24, 25, 26, 27, 28, 29, 30, 31)
NORM2_AT = ((27, 29), (31, 32))
H2T_AT = (31, 34)
GATE_AT = (35,)
HALF_AT = (32, 33, 34, 34)
UPDOWN_AT = (36, 37, 38, 38, 39, 40, 40, 41, 42, 43, 44)
MIXING = ((0, 0, 0), (0, 1, 3), (3, 4, 6), (6, 7, 9), (9, 10, 12), (12, 13, 15), (15, 16, 16)) + ((16, 16, 16),) * (JT - 7)
MIXT_AT = (41, 41)
MIX_AT = (42, 42, 43, 43, 44, 45)
DOWN_AT = (44, 45, 46, 47)
O_PARTS = len(OPROJ_AT) // T
KINDS = (("qkv", QKV_AT), ("turn", TURN_AT), ("score", SCORE_AT), ("probT", PROBT_AT), ("av", AV_AT),
         ("oproj", OPROJ_AT[::O_PARTS]), ("h2T", H2T_AT), ("gate", GATE_AT), ("updown", HALF_AT + UPDOWN_AT[len(HALF_AT):]),
         ("mixT", MIXT_AT), ("mix", MIX_AT), ("down", DOWN_AT[:T]))
assert all(SUM_AT[n] > SCORE_AT[n] and PROBT_AT[n] > SUM_AT[n] for n in range(3 * HKV))
assert all(AV_AT[2 * g] > PROBT_AT[3 * g] and AV_AT[2 * g + 1] > PROBT_AT[3 * g + 2] for g in range(HKV))
assert all(MIX_AT[p] >= UPDOWN_AT[min(2 * p + 1, JT - 1)] for p in range(len(MIX_AT)))
assert MIXT_AT[0] > UPDOWN_AT[6]


def work(s):
    return [(kind, n) for kind, steps in KINDS for n, at in enumerate(steps) if at == s]


def use(s):
    w = [x for x in work(s) if x[0] not in ("oproj", "down", "updown")]
    w += [("updown", n) for n, at in enumerate(UPDOWN_AT) if at == s]
    w += [("oproj", n) for n, at in enumerate(OPROJ_AT[O_PARTS - 1::O_PARTS]) if at == s]
    w += [("down", n) for n, at in enumerate(DOWN_AT[-T:]) if at == s]
    return w


def units(l, a):
    return [k for k, at in enumerate(UNIT_AT[l]) if at == a]


def done(l, t):
    return UNIT_AT[l][NU // T * (t + 1) - 1] + PV_LAG


def summed(s):
    return [n for n, at in enumerate(SUM_AT) if at == s]


SLOW = [("score", n) for n in range(3 * HKV)] + [("updown", n) for n in range(JT) if n not in (2, 3)] + [("qkv", n) for n in range(5)]
SLOW_BANKS, QUICK_BANKS = 2, 3
BANKS = SLOW_BANKS + QUICK_BANKS
ORDER = [w for s in range(STEPS) for w in work(s)]
PLACE, FILLS = {}, {}
for first, banks, fills in ((0, SLOW_BANKS, [w for w in ORDER if w in SLOW]),
                            (SLOW_BANKS, QUICK_BANKS, [w for w in ORDER if w not in SLOW])):
    assert len(fills) % banks == 0
    for n, w in enumerate(fills):
        PLACE[w] = (first + n % banks, n // banks)
    for k in range(banks):
        FILLS[first + k] = len(fills) // banks


def block_program(nc, x, ctxT, w0, w1, gat_rows, norm_cols, qk_rows, wqkv, wo, wgate, wgu, wd, consts, spread, out):
    ctx = ExitStack()
    with ctx:
        def sb(name, shape, dt=F32):
            return ctx.enter_context(nc.sbuf_tensor(name, shape, dt))

        def pb(name, shape, dt=F32):
            return ctx.enter_context(nc.psum_tensor(name, shape, dt))

        def sem(name):
            return ctx.enter_context(nc.semaphore(name))

        cst = sb("cst", [P, C_END])
        ident = cst[:, C_ID:C_ID + P]
        identb = sb("identb", [P, P], BF16)
        causal = sb("causal", [P, P], BF16)
        expert_rows = sb("expert_rows", [NP * E, EI], BF16)
        rows = sb("rows", [P, 6 * D])
        w0x = sb("w0x", [F_IN, D + 2 * H])
        w1x = sb("w1x", [P, KT, D + 2 * H])
        cols = sb("cols", [P, 2 * KT])
        qkw = sb("qkw", [P, 2 * HD])
        rope_c = sb("rope_c", [P, 2, T, HD])
        rope_s = sb("rope_s", [P, 2, T, HD])
        wqkv_sb = sb("wqkv_sb", [P, KT, (HQ + 2 * HKV) * HD])
        wo_sb = sb("wo_sb", [P, HQ, D])
        wgate_sb = sb("wgate_sb", [P, KT, E])
        wgu_sb = sb("wgu_sb", [P, 2, KT, EI])
        wd_sb = sb("wd_sb", [P, JT, D])
        xin = sb("xin", [P, T, D])
        cin = sb("cin", [F_IN, N])
        stats = sb("stats", [P, T, 6])
        mv = sb("mv", [P, T, 2])
        rs_v = sb("rs_v", [P, 2 * T])
        rs_y = sb("rs_y", [P, 2 * T])
        rs_a = sb("rs_a", [P, 2 * T])
        maskv = sb("maskv", [P, T, N])
        feat = sb("feat", [P, T, H, FE])
        sn_res = sb("sn_res", [P, T, 2 * H])
        parts = sb("parts", [P, T, NP, 2 * H], BF16)
        partsT = sb("partsT", [KZ, N], BF16)
        pair_l = sb("pair_l", [KZ, N], BF16)
        pair_r = sb("pair_r", [KZ, H, N], BF16)
        zs = sb("zs", [P, 2, 2 * N])
        lr = sb("lr", [P, 2, 2 * N])
        tt = sb("tt", [P, 3, 2, N])
        gmn = sb("gmn", [P, 3, 2])
        gpT = sb("gpT", [P, 3, 2, T, P])
        gsum = sb("gsum", [P, H])
        go = rows[:, 2 * D:4 * D].rearrange("p (t d) -> p t d", t=T)
        gex = sb("gex", [P, T, D])
        wprod = gex[:, 0, :]
        x1 = sb("x1", [P, T, D])
        hid = sb("hid", [P, T, D])
        hn = gex
        hT = sb("hT", [P, KT, N])
        gT = hT
        early = sb("early", [P, 6, G * HD])[:, :, :]
        raw, sq = early[:, 0:3, :], early[:, 3:6, :]
        v_sb = sb("v_sb", [P, T, HKV * HD])
        m1 = sb("m1", [P, 4, G * HD])
        m2 = sb("m2", [P, 4, G * HD])
        ssq = sb("ssq", [P, QU * G])
        rms = sb("rms", [P, QU * G])
        rms_a = sb("rms_a", [P, QU * G])
        h2_v = sb("h2_v", [P, T])
        h2_m = sb("h2_m", [P, T])
        h2_y = sb("h2_y", [P, T])
        h2_a = sb("h2_a", [P, T])
        qT = sb("qT", [P, HQ, N])
        kT = sb("kT", [P, HKV, N])
        smx = sb("smx", [P, 3 * HKV, G])
        sneg = sb("sneg", [P, 3 * HKV, G])
        ssum = sb("ssum", [P, 3 * HKV, G])
        srcp = sb("srcp", [P, 3 * HKV, G])
        prob = sb("prob", [P, 5, 2 * N])
        pT0 = sb("pT0", [P, G, P])
        pT1 = sb("pT1", [P, T, G, P])
        oT = qT
        late = m1[:, :, :].rearrange("p a (t d) -> p a t d", t=T)
        hid2, osum, h2n = late[:, 0], late[:, 1], late[:, 2]
        ss2 = sb("ss2", [P, T])
        tokT = late[:, 3]
        lg = sb("lg", [P, T, E])
        lmx = sb("lmx", [P, T])
        lex = sb("lex", [P, T, E])
        spare = pT0[:, :, :].rearrange("p h q -> p (h q)")
        cmp1 = spare[:, N:N + T * E * E].rearrange("p (t e j) -> p t e j", t=T, e=E)
        cmp2 = spare[:, N + T * E * E:N + 2 * T * E * E].rearrange("p (t e j) -> p t e j", t=T, e=E)
        rank = sb("rank", [P, T, E])
        mixp = sb("mixp", [P, T, NP, E], BF16)
        mixT = sb("mixT", [NP * E, N], BF16)
        th = pT1[:, :, :, :].rearrange("p m h q -> p (m h q)")[:, 0:3 * N].rearrange("p (a n) -> p a n", a=3)
        ga = spare[:, 0:N]
        ah = early.rearrange("p a c -> p (a c)")[:, 0:JT * N].rearrange("p (j n) -> p j n", j=JT)
        yo = rows[:, 0:T * D].rearrange("p (t d) -> p t d", t=T)
        spread_in = ah[0:NP * E, :, :].rearrange("p j n -> p (j n)")[:, 0:EI]

        zb = pb("zb", [P, 512])
        tb = pb("tb", [P, 512])
        ob = pb("ob", [P, 512])
        bank = [pb(f"bank{k}", [P, 512]) for k in range(BANKS)]

        in_cst, in_w0, in_gat, in_x, in_c = sem("in_cst"), sem("in_w0"), sem("in_gat"), sem("in_x"), sem("in_c")
        in_qkv, in_o, in_gu, in_d = sem("in_qkv"), sem("in_o"), sem("in_gu"), sem("in_d")
        out_free = sem("out_free")
        x_used, c_used = sem("x_used"), sem("c_used")
        setup_v, setup_done = sem("setup_v"), sem("setup_done")
        dve_a = sem("dve_a")
        z_full, z_free = sem("z_full"), sem("z_free")
        t_full, t_free = sem("t_full"), sem("t_free")
        parts_ready, pair_l_ready = sem("parts_ready"), sem("pair_l_ready")
        pair_r0_ready, pair_r1_ready = sem("pair_r0_ready"), sem("pair_r1_ready")
        lrelu_done, score_ready, shifted = sem("lrelu_done"), sem("score_ready"), sem("shifted")
        pv_done, o_free = sem("pv_done"), sem("o_free")
        gout_ready, gexp_ready, gres_ready, hn_ready = sem("gout_ready"), sem("gexp_ready"), sem("gres_ready"), sem("hn_ready")
        ln_seed, pool_a, ln_ready, hid_ready = sem("ln_seed"), sem("pool_a"), sem("ln_ready"), sem("hid_ready")
        dve_b = sem("dve_b")
        full = [sem(f"full{k}") for k in range(BANKS)]
        free = [sem(f"free{k}") for k in range(BANKS)]
        raw_ready, m1_ready, m2_ready = sem("raw_ready"), sem("m1_ready"), sem("m2_ready")
        k_ready, seed_ready, rms_ready, pool_b = sem("k_ready"), sem("seed_ready"), sem("rms_ready"), sem("pool_b")
        sneg_ready, srcp_ready, prob_ready = sem("sneg_ready"), sem("srcp_ready"), sem("prob_ready")
        hid2_ready, osum_ready, h2n_ready = sem("hid2_ready"), sem("osum_ready"), sem("h2n_ready")
        lneg_ready, lexp_ready, mix_ready, tanh_ready, y_ready = sem("lneg_ready"), sem("lexp_ready"), sem("mix_ready"), sem("tanh_ready"), sem("y_ready")

        block = ctx.enter_context(nc.Block())

        def z_value(b, l, n):
            return b * 2 * (NU + 1) + l * (NU + 1) + n + 1

        def t_value(b, l, n):
            return b * 2 * (NU + 3) + l * (NU + 3) + n + 1

        def unit(b, l, k):
            return b * 2 * NU + l * NU + k

        def rq(g, t, h, n=1):
            at = (2 + 2 * g + t) * G + h
            return rms[:, at:at + n]

        def filled(eng, b, w):
            k, i = PLACE[w]
            eng.wait_ge(full[k], b * FILLS[k] + i + 1)

        def emptied(eng, b, w):
            k, i = PLACE[w]
            eng.wait_ge(free[k], b * FILLS[k] + i + 2)

        def emptied_all(eng, b, ws):
            last = {}
            for w in ws:
                last[PLACE[w][0]] = w
            for w in last.values():
                emptied(eng, b, w)

        def bank_of(w):
            return bank[PLACE[w][0]]

        def full_of(w):
            return full[PLACE[w][0]]

        def free_of(w):
            return free[PLACE[w][0]]

        @block.sync
        def _(sp):
            sp.dma_start(w0x[:, 0:D], w0).then_inc(in_w0, 16)
            sp.dma_start(rows[:, 0:2 * D], gat_rows[:, 0:2 * D]).then_inc(in_w0, 16)
            sp.dma_start(cst[:, :], consts).then_inc(in_cst, 16)
            sp.dma_start(cin[:, :], ctxT[0]).then_inc(in_c, 16)
            sp.dma_start(xin[:, :, :], x[0].rearrange("(t p) d -> p t d", p=P)).then_inc(in_x, 16)
            sp.dma_start(rows[:, 2 * D:6 * D], gat_rows[:, 2 * D:6 * D]).then_inc(in_gat, 16)
            sp.dma_start(w1x[:, :, 0:D], w1.rearrange("(k p) n -> p k n", p=P)).then_inc(in_gat, 16)
            sp.dma_start(spread_in, spread).then_inc(in_gat, 16)
            sp.dma_start(cols[:, :], norm_cols).then_inc(in_gat, 16)
            sp.dma_start(qkw[:, :], qk_rows).then_inc(in_gat, 16)
            sp.dma_start(wqkv_sb[:, :, :], wqkv.rearrange("(k p) n -> p k n", p=P)).then_inc(in_qkv, 16)
            sp.dma_start(wo_sb[:, :, :], wo.rearrange("(h p) n -> p h n", p=P)).then_inc(in_o, 16)
            sp.dma_start(wgate_sb[:, :, :], wgate.rearrange("(k p) n -> p k n", p=P)).then_inc(in_gu, 16)
            for m in range(2):
                sp.dma_start(wgu_sb[:, m, :, :], wgu[m].rearrange("(k p) n -> p k n", p=P)).then_inc(in_gu, 16)
            sp.dma_start(wd_sb[:, :, :], wd.rearrange("(j p) n -> p j n", p=P)).then_inc(in_d, 16)

            def load_inputs(b):
                sp.wait_ge(c_used, b)
                sp.dma_start(cin[:, :], ctxT[bass.ds(b, 1)].squeeze(0) if not isinstance(b, int) else ctxT[b]).then_inc(in_c, 16)
                sp.wait_ge(x_used, b)
                src = x[bass.ds(b, 1)].squeeze(0) if not isinstance(b, int) else x[b]
                sp.dma_start(xin[:, :, :], src.rearrange("(t p) d -> p t d", p=P)).then_inc(in_x, 16)

            def store(b):
                dst = out[bass.ds(b, 1)].squeeze(0) if not isinstance(b, int) else out[b]
                for t in range(T):
                    sp.wait_ge(y_ready, b * T + t + 1)
                    sp.dma_start(dst[t * P:(t + 1) * P, :], yo[:, t, :]).then_inc(out_free, 16)

            load_inputs(1)
            with sp.Fori(0, B - 2) as b:
                load_inputs(b + 2)
                store(b)
            store(B - 2)
            store(B - 1)
            sp.wait_ge(out_free, 16 * T * (B + 1))

        @block.tensor
        def _(pe):
            def gat(b, a):
                for l in range(2):
                    operands = [(cin, w0x)] if l == 0 else [(gT[:, k, :], w1x[:, k, :]) for k in range(KT)]
                    if a == TERMS_AT[l]:
                        if l == 0:
                            pe.wait_ge(in_c, (b + 1) * 16)
                        else:
                            pe.wait_ge(t_free, t_value(b, 0, NU + 2) + 1)
                            pe.nop(nofuse=True)
                        pe.wait_ge(t_free, t_value(b, l, 0))
                        for t in range(T):
                            for i, (xt, w) in enumerate(operands):
                                mm = pe.matmul(tb[:, t * 2 * H:(t + 1) * 2 * H], xt[:, t * P:(t + 1) * P], w[:, D:D + 2 * H],
                                               start=(i == 0), stop=(i == len(operands) - 1))
                        mm.then_inc(t_full, 1)
                    if a == PARTS_AT[l]:
                        pe.wait_ge(parts_ready, b * 2 + l + 1)
                        pe.wait_ge(t_free, t_value(b, l, 1))
                        pe.nop(nofuse=True)
                        for t in range(T):
                            mm = pe.transpose(tb[0:KZ, t * P // 2:(t + 1) * P // 2].bitcast(BF16),
                                              parts[:, t, :, :].rearrange("p a c -> p (a c)"), identb[:, :])
                        mm.then_inc(t_full, 1)
                        pe.wait_ge(z_free, z_value(b, l, 0))
                        for t in range(T):
                            for i, (xt, w) in enumerate(operands):
                                mm = pe.matmul(zb[:, t * D:(t + 1) * D], xt[:, t * P:(t + 1) * P], w[:, 0:D],
                                               start=(i == 0), stop=(i == len(operands) - 1))
                        mm.then_inc(z_full, 1)
                    for k in units(l, a):
                        t, hp = divmod(k, H // 2)
                        if k == 0:
                            pe.wait_ge(pair_l_ready, b * 2 + l + 1)
                        if k < H // 2:
                            pe.wait_ge(pair_r0_ready if k < 2 else pair_r1_ready, b * 4 + l * 2 + k % 2 + 1)
                        pe.wait_ge(z_free, z_value(b, l, k + 1))
                        pe.matmul(zb[:, :], pair_l[:, t * P:(t + 1) * P],
                                  pair_r[:, 2 * hp:2 * hp + 2, :].rearrange("k h m -> k (h m)"), start=True, stop=True)\
                          .then_inc(z_full, 1)
                    for k in units(l, a - TRANS_LAG):
                        pe.wait_ge(shifted, unit(b, l, k) + 1)
                        pe.wait_ge(t_free, t_value(b, l, k + 2))
                        for h in range(2):
                            for m in range(T):
                                mm = pe.transpose(tb[:, (h * T + m) * P:(h * T + m + 1) * P],
                                                  tt[:, k % 3, h, m * P:(m + 1) * P], ident)
                        mm.then_inc(t_full, 1)
                    for k in units(l, a - PV_LAG):
                        t, hp = divmod(k, H // 2)
                        pe.wait_ge(t_free, t_value(b, l, k + 2) + 1)
                        if hp == 0:
                            pe.wait_ge(o_free, b * 2 * T + l * T + t + 1)
                        for h in range(2):
                            hh = 2 * hp + h
                            for m in range(T):
                                mm = pe.matmul(ob[:, hh * FE:(hh + 1) * FE], gpT[:, k % 3, h, m, :], feat[:, m, hh, :],
                                               start=(m == 0), stop=(m == T - 1))
                        mm.then_inc(pv_done, 1)
                if a in (OUT_AT, HN_AT):
                    l = 0 if a != HN_AT else 1
                    if l == 0:
                        pe.wait_ge(gres_ready, (b + 1) * T)
                    else:
                        pe.wait_ge(hn_ready, b + 1)
                    pe.wait_ge(t_free, t_value(b, l, NU + 2))
                    for k in range(KT):
                        for t in range(T):
                            mm = pe.transpose(tb[:, (k * T + t) * P:(k * T + t + 1) * P], gex[:, t, k * P:(k + 1) * P], ident)
                    mm.then_inc(t_full, 1)

            def experts_in(n, c0, c1):
                ps = bank_of(("updown", n))
                for m in range(2):
                    for k in range(KT):
                        mm = pe.matmul(ps[:, m * N + c0:m * N + c1], wgu_sb[:, m, k, n * P:(n + 1) * P], tokT[:, k, c0:c1],
                                       start=(k == 0), stop=(k == KT - 1))
                return mm

            def fill(b, w):
                kind, n = w
                ps = bank_of(w)
                bk, turn = PLACE[w]
                if kind == "qkv" and n == 0:
                    pe.wait_ge(t_free, t_value(b, 1, NU + 2) + 1)
                if kind == "turn":
                    if n < T:
                        pe.wait_ge(k_ready, (b + 1) * T)
                    else:
                        pe.wait_ge(m1_ready, b * QU + n + 4)
                        pe.wait_ge(m2_ready, b * QU + n + 4)
                if kind == "score":
                    g, j = divmod(n, 3)
                    t = min(j, 1)
                    emptied_all(pe, b, [("turn", t), ("turn", 2 + 2 * g + t)])
                if kind == "probT":
                    pe.wait_ge(prob_ready, b * 3 * HKV + n + 1)
                if kind == "av":
                    g, t = divmod(n, 2)
                    emptied_all(pe, b, [("probT", 3 * g + j) for j in ([0] if t == 0 else [1, 2])])
                if kind == "oproj":
                    emptied_all(pe, b, [("av", 2 * g + n) for g in range(HKV)])
                if kind == "h2T":
                    pe.wait_ge(h2n_ready, b * T + n + 1)
                if kind == "updown":
                    emptied(pe, b, ("h2T", 0 if n < len(HALF_AT) else T - 1))
                if kind == "gate":
                    emptied_all(pe, b, [("h2T", t) for t in range(T)])
                if kind == "mixT":
                    pe.wait_ge(mix_ready, b + 1)
                if kind == "mix":
                    emptied_all(pe, b, [("mixT", t) for t in range(T)])
                if kind == "down":
                    emptied_all(pe, b, [("mix", p) for p in range(3)])
                if kind in ("score", "av", "oproj", "gate", "updown", "mix", "down"):
                    pe.nop(nofuse=True)
                pe.wait_ge(free[bk], b * FILLS[bk] + turn + 1)

                if kind == "qkv":
                    c, t = (HKV, n) if n < 2 else (HKV + 1, n - 2) if n < 4 else divmod(n - 4, 2)
                    for k in range(KT):
                        mm = pe.matmul(ps[:, :], hT[:, k, t * P:(t + 1) * P], wqkv_sb[:, k, c * G * HD:(c + 1) * G * HD],
                                       start=(k == 0), stop=(k == KT - 1))
                elif kind == "turn":
                    for h in range(G):
                        src, dst = (slice(h * HD, (h + 1) * HD)), ps[:, h * P:(h + 1) * P]
                        if n < T:
                            mm = pe.transpose(dst, m1[:, n % 4, src], ident)
                        else:
                            pe.matmul(dst, m1[:, n % 4, src], ident, is_transpose=True, start=True, stop=False)
                            mm = pe.matmul(dst, m2[:, n % 4, src], ident, is_transpose=True, start=False, stop=True)
                elif kind == "score":
                    nk = P * (t + 1)
                    heads = range(G) if t == 0 else range(2 * (j - 1), 2 * (j - 1) + 2)
                    for i, h in enumerate(heads):
                        pe.matmul(ps[:, i * nk:(i + 1) * nk], qT[:, G * g + h, t * P:(t + 1) * P], kT[:, g, 0:nk],
                                  start=True, stop=False)
                        mm = pe.matmul(ps[:, (i + 1) * nk - P:(i + 1) * nk], identb[:, :], causal[:, :], start=False, stop=True)
                elif kind == "probT":
                    g, j = divmod(n, 3)
                    if j == 0:
                        for h in range(G):
                            mm = pe.transpose(ps[:, h * P:(h + 1) * P], prob[:, n % 5, h * P:(h + 1) * P], ident)
                    else:
                        for m in range(T):
                            for h in range(2):
                                mm = pe.transpose(ps[:, (m * 2 + h) * P:(m * 2 + h + 1) * P],
                                                  prob[:, n % 5, h * N + m * P:h * N + (m + 1) * P], ident)
                elif kind == "av":
                    if t == 0:
                        mm = pe.matmul(ps[:, :], v_sb[:, 0, g * HD:(g + 1) * HD], pT0[:, :, :].rearrange("p h q -> p (h q)"),
                                       start=True, stop=True)
                    else:
                        for m in range(T):
                            mm = pe.matmul(ps[:, :], v_sb[:, m, g * HD:(g + 1) * HD],
                                           pT1[:, m, :, :].rearrange("p h q -> p (h q)"), start=(m == 0), stop=(m == T - 1))
                elif kind == "h2T":
                    for k in range(KT):
                        mm = pe.transpose(ps[:, k * P:(k + 1) * P], h2n[:, n, k * P:(k + 1) * P], ident)
                elif kind == "gate":
                    for t in range(T):
                        for k in range(KT):
                            mm = pe.matmul(ps[:, t * E:(t + 1) * E], tokT[:, k, t * P:(t + 1) * P], wgate_sb[:, k, :],
                                           start=(k == 0), stop=(k == KT - 1))
                elif kind == "updown":
                    mm = experts_in(n, 0, P if n < len(HALF_AT) else N)
                elif kind == "mixT":
                    mm = pe.transpose(ps[0:NP * E, 0:P // 2].bitcast(BF16), mixp[:, n, :, :].rearrange("p a e -> p (a e)"), identb[:, :])
                elif kind == "mix":
                    for i, j in enumerate(range(2 * n, min(2 * n + 2, JT))):
                        mm = pe.matmul(ps[:, i * N:(i + 1) * N], expert_rows[:, j * P:(j + 1) * P], mixT[:, :], start=True, stop=True)
                if kind not in ("oproj", "down") and not (kind == "updown" and n < len(HALF_AT)):
                    mm.then_inc(full[bk], 1)

            def product(w, t, lhs, rhs, k0, k1, end):
                for k in range(k0, k1):
                    mm = pe.matmul(bank_of(w)[:, 0:D], lhs[:, k, t * P:(t + 1) * P], rhs[:, k, :], start=(k == 0), stop=(k == end - 1))
                if k1 == end:
                    mm.then_inc(full_of(w), 1)

            def long_products(b, s):
                for n in [n for n, at in enumerate(OPROJ_AT) if at == s]:
                    t, part = divmod(n, O_PARTS)
                    product(("oproj", t), t, oT, wo_sb, part * HQ // O_PARTS, (part + 1) * HQ // O_PARTS, HQ)
                for n in [n for n, at in enumerate(UPDOWN_AT[:len(HALF_AT)]) if at == s]:
                    emptied(pe, b, ("h2T", T - 1))
                    pe.nop(nofuse=True)
                    experts_in(n, P, N).then_inc(full_of(("updown", n)), 1)
                for n in [n for n, at in enumerate(DOWN_AT) if at == s]:
                    part, t = divmod(n, T)
                    if t == 0 and part == 1:
                        emptied_all(pe, b, [("mix", p) for p in range(3, (JT + 1) // 2)])
                    product(("down", t), t, ah, wd_sb, *((0, 6), (6, JT))[part], JT)

            pe.wait_ge(in_cst, 16)
            pe.wait_ge(setup_done, 1)
            for s in range(STEPS):
                if s == TERMS_AT[1]:
                    pe.wait_ge(setup_done, 2)
                gat(0, s)
            pe.wait_ge(setup_done, 3)
            pe.wait_ge(in_qkv, 16)
            pe.wait_ge(in_o, 16)
            pe.wait_ge(in_gu, 48)
            pe.wait_ge(in_d, 16)
            with pe.Fori(0, B - 1) as b:
                for s in range(STEPS):
                    gat(b + 1, s)
                    for w in work(s):
                        fill(b, w)
                    long_products(b, s)
            for s in range(STEPS):
                for w in work(s):
                    fill(B - 1, w)
                long_products(B - 1, s)

        @block.scalar
        def _(act):
            def gat(b, a):
                for l in range(2):
                    if a == PARTS_AT[l]:
                        act.wait_ge(z_full, z_value(b, l, 0))
                        act.activation(feat[:, :, :, 0:FO], zb[:, :].rearrange("p (t h o) -> p t h o", t=T, h=H), ACT.Copy)\
                           .then_inc(z_free, 1)
                    if a == PAIRS_AT[l]:
                        act.wait_ge(pair_l_ready, b * 2 + l + 1)
                        for h in range(H // 2):
                            ins = act.activation(pair_r[:, h, :], partsT[:, :], ACT.Identity, bias=cst[0:KZ, C_ONE + h:C_ONE + h + 1],
                                                 scale=cst[0:KZ, C_PICK + h:C_PICK + h + 1])
                            if h % 2:
                                ins.then_inc(pair_r0_ready, 1)
                    for k in units(l, a):
                        act.wait_ge(z_full, z_value(b, l, k + 1))
                        act.wait_ge(lrelu_done, unit(b, l, k) + 1)
                        act.activation(zs[:, k % 2, :], zb[:, :], ACT.Copy, scale=-1.0).then_inc(z_free, 1)
                    for k in units(l, a - TRANS_LAG):
                        act.wait_ge(t_full, t_value(b, l, k + 2))
                        if k >= 3:
                            act.wait_ge(pv_done, unit(b, l, k) - 2)
                        act.activation(gpT[:, k % 3, :, :, :].rearrange("p h m i -> p (h m i)"), tb[:, :], ACT.Exp).then_inc(t_free, 1)
                    for t in range(T):
                        if a == done(l, t) + ELU_LAG:
                            act.wait_ge(gout_ready, b * 2 * T + l * T + t + 1)
                            act.activation(gex[:, t, :], go[:, t, :], ACT.Exp).then_inc(gexp_ready, 1)

            def empty(b, w):
                kind, n = w
                ps = bank_of(w)
                if kind == "qkv":
                    filled(act, b, w)
                    if n in (2, 3):
                        act.activation(v_sb[:, n - 2, :], ps[:, :], ACT.Copy).then_inc(free_of(w), 1)
                    else:
                        u = n if n < 2 else n - 2
                        act.wait_ge(m1_ready, b * QU + u + 1)
                        act.wait_ge(m2_ready, b * QU + u + 1)
                        act.activation(raw[:, u % 3, :], ps[:, :], ACT.Copy).then_inc(raw_ready, 1)
                        act.activation(sq[:, u % 3, :], ps[:, :], ACT.Square).then_inc(free_of(w), 1)
                elif kind == "turn":
                    filled(act, b, w)
                    if n < 2:
                        dst = kT[:, :, n * P:(n + 1) * P]
                    else:
                        g, t = divmod(n - 2, 2)
                        dst = qT[:, G * g:G * g + G, t * P:(t + 1) * P]
                    act.activation(dst, ps[:, :].rearrange("p (h q) -> p h q", h=G), ACT.Copy).then_inc(free_of(w), 1)
                elif kind == "score":
                    g, j = divmod(n, 3)
                    t = min(j, 1)
                    nk = P * (t + 1)
                    heads = range(G) if t == 0 else range(2 * (j - 1), 2 * (j - 1) + 2)
                    act.wait_ge(sneg_ready, b * 3 * HKV + n + 1)
                    if n >= 5:
                        filled(act, b, ("probT", n - 5))
                    for i, h in enumerate(heads):
                        ins = act.activation(prob[:, n % 5, i * nk:(i + 1) * nk], ps[:, i * nk:(i + 1) * nk], ACT.Exp,
                                             bias=sneg[:, n, i:i + 1], scale=rq(g, t, h), accum_out=ssum[:, n, i:i + 1])
                    ins.then_inc(free_of(w), 1)
                elif kind == "av":
                    g, t = divmod(n, 2)
                    filled(act, b, w)
                    act.activation(oT[:, G * g:G * g + G, t * P:(t + 1) * P], ps[:, :].rearrange("p (h q) -> p h q", h=G), ACT.Copy)\
                       .then_inc(free_of(w), 1)
                elif kind == "gate":
                    for t in range(T):
                        act.wait_ge(lneg_ready, b * T + t + 1)
                        act.activation(lex[:, t, :], lg[:, t, :], ACT.Exp, bias=lmx[:, t:t + 1]).then_inc(lexp_ready, 1)
                elif kind == "updown":
                    filled(act, b, w)
                    if n >= 3:
                        emptied(act, b, ("updown", n - 3))
                    act.activation(th[:, n % 3, :], ps[:, 0:N], ACT.Tanh, scale=0.5).then_inc(tanh_ready, 1)

            for s in range(STEPS):
                gat(0, s)
            act.wait_ge(setup_done, 3)
            with act.Fori(0, B - 1) as b:
                for s in range(STEPS):
                    gat(b + 1, s)
                    for w in use(s):
                        empty(b, w)
            for s in range(STEPS):
                for w in use(s):
                    empty(B - 1, w)

        @block.gpsimd
        def _(pool):
            links, links_a = [0], [0]

            def link(b, ins):
                links[0] += 1
                ins.then_inc(pool_b, 1)
                pool.wait_ge(pool_b, b * N_P + links[0])

            def link_a(b, ins):
                links_a[0] += 1
                ins.then_inc(pool_a, 1)
                pool.wait_ge(pool_a, b * 12 + links_a[0])

            def newton(link, b, y, a, v):
                link(b, pool.tensor_tensor(a, y, y, ALU.mult))
                link(b, pool.tensor_tensor(a, a, v, ALU.mult))
                pool.nop(nofuse=True)
                link(b, pool.tensor_scalar(a, a, -0.5, 1.5, ALU.mult, ALU.add))
                link(b, pool.tensor_tensor(y, y, a, ALU.mult))

            def gat(b, a):
                for l in range(2):
                    if a == PAIRS_AT[l]:
                        pool.wait_ge(pair_l_ready, b * 2 + l + 1)
                        pool.nop(nofuse=True)
                        for h in range(H // 2, H):
                            ins = pool.tensor_scalar(pair_r[:, h, :], partsT[:, :], cst[0:KZ, C_PICK + h:C_PICK + h + 1],
                                                     cst[0:KZ, C_ONE + h:C_ONE + h + 1], ALU.mult, ALU.add)
                            if h % 2:
                                ins.then_inc(pair_r1_ready, 1)
                    for k in units(l, a - SCORE_LAG):
                        pool.wait_ge(score_ready, unit(b, l, k) + 1)
                        pool.nop(nofuse=True)
                        for h in range(2):
                            ins = pool.tensor_scalar(tt[:, k % 3, h, :], tt[:, k % 3, h, :], -1.0, gmn[:, k % 3, h:h + 1],
                                                     ALU.mult, ALU.add)
                        ins.then_inc(shifted, 1)

                if a == LN2_AT[1]:
                    pool.wait_ge(ln_seed, b + 1)
                    pool.nop(nofuse=True)
                    links_a[0] = 0
                    for _ in range(3):
                        newton(link_a, b, rs_y[:, :], rs_a[:, :], rs_v[:, :])
                    pool.sem_inc(ln_ready, 1)
                    for t in range(T):
                        ins = pool.tensor_scalar(hid[:, t, :], x1[:, t, :], mv[:, t, 0:1], rs_y[:, t:t + 1], ALU.subtract, ALU.mult)
                    ins.then_inc(hid_ready, 1)

            def inverse_rms(b, c):
                lo, hi = ((0, 2 * G), (2 * G, 6 * G), (6 * G, 10 * G))[c]
                v, y, a = ssq[:, lo:hi], rms[:, lo:hi], rms_a[:, lo:hi]
                pool.wait_ge(seed_ready, b * 3 + c + 1)
                for _ in range(3):
                    newton(link, b, y, a, v)
                if c == 0:
                    pool.sem_inc(rms_ready, 1)
                else:
                    pool.nop(nofuse=True)
                    pool.tensor_scalar(y, y, SCALE, 1.0, ALU.mult, ALU.mult).then_inc(rms_ready, 1)

            def part(b, w):
                kind, n = w
                if kind == "qkv" and n not in (2, 3):
                    u = n if n < 2 else n - 2
                    which, t = (1, u) if u < 2 else (0, u % 2)
                    pool.wait_ge(raw_ready, b * QU + u + 1)
                    if u >= 4:
                        filled(pool, b, ("turn", u - 4))
                    src = raw[:, u % 3, :].rearrange("p (h c d) -> p h c d", h=G, c=2)
                    dst = m2[:, u % 4, :].rearrange("p (h c d) -> p h c d", h=G, c=2)
                    for c in range(2):
                        s_ = rope_s[:, which, t, c * HD // 2:(c + 1) * HD // 2].unsqueeze(1).broadcast_to([P, G, HD // 2])
                        ins = pool.tensor_tensor(dst[:, :, c, :], src[:, :, 1 - c, :], s_, ALU.mult)
                    ins.then_inc(m2_ready, 1)
                    if u in (1, 5, 9):
                        inverse_rms(b, (u - 1) // 4)
                elif kind == "oproj":
                    pool.wait_ge(hid2_ready, b * T + n + 1)
                    pool.tensor_tensor(osum[:, n, :], x1[:, n, :], hid2[:, n, :], ALU.add).then_inc(osum_ready, 1)

            def normalise(b, s):
                for n in summed(s):
                    nh, nk = (G, P) if n % 3 == 0 else (2, N)
                    pool.wait_ge(srcp_ready, b * 3 * HKV + n + 1)
                    pool.nop(nofuse=True)
                    for i in range(nh):
                        part_ = prob[:, n % 5, i * nk:(i + 1) * nk]
                        ins = pool.tensor_scalar(part_, part_, srcp[:, n, i:i + 1], 1.0, ALU.mult, ALU.mult)
                    ins.then_inc(prob_ready, 1)

            pool.wait_ge(setup_done, 1)
            for s in range(STEPS):
                gat(0, s)
            pool.wait_ge(setup_done, 3)
            with pool.Fori(0, B - 1) as b:
                links[0] = 0
                for s in range(STEPS):
                    gat(b + 1, s)
                    for w in use(s):
                        part(b, w)
                    normalise(b, s)
            assert links[0] == N_P, links
            links[0] = 0
            for s in range(STEPS):
                for w in use(s):
                    part(B - 1, w)
                normalise(B - 1, s)

        A_LINKS, B_LINKS = [0], [0]

        @block.vector
        def _(dve):
            count = [0, 0]
            mixed = [0]

            def link_a(b, ins):
                count[0] += 1
                ins.then_inc(dve_a, 1)
                dve.wait_ge(dve_a, b * N_A + count[0])

            def link_b(b, ins):
                count[1] += 1
                ins.then_inc(dve_b, 1)
                dve.wait_ge(dve_b, b * N_B + count[1])

            def mark_b(ins):
                count[1] += 1
                ins.then_inc(dve_b, 1)
                return count[1]

            def first_guess(link, b, y, a, v):
                link(b, dve.tensor_scalar(a.bitcast(I32), v.bitcast(I32), 1, None, ALU.logical_shift_right))
                link(b, dve.tensor_scalar(y.bitcast(I32), a.bitcast(I32), -1, MAGIC, ALU.mult, ALU.add))

            def newton(link, b, y, a, v):
                link(b, dve.scalar_tensor_tensor(a, y, -0.5, y, ALU.mult, ALU.mult))
                link(b, dve.tensor_tensor(a, a, v, ALU.mult))
                link(b, dve.scalar_tensor_tensor(y, a, 1.5, y, ALU.add, ALU.mult))

            def moments(b):
                dve.nop(nofuse=True)
                for t in range(T):
                    ins = dve.bn_aggr(mv[:, t, :], stats[:, t, :])
                link_a(b, ins)

            def gat(b, a):
                if a == MASK_AT[0]:
                    dve.wait_ge(in_x, (b + 1) * 16)
                    if not isinstance(b, int):
                        dve.wait_ge(hid_ready, b)
                    for t in range(T):
                        ins = dve.bn_stats(stats[:, t, :], xin[:, t, :])
                    link_a(b, ins)
                    moments(b)
                    link_a(b, dve.tensor_scalar(rs_v[:, 0:T], mv[:, :, 1], LN_EPS, None, ALU.add))
                    first_guess(link_a, b, rs_y[:, 0:T], rs_a[:, 0:T], rs_v[:, 0:T])
                if a in MASK_AT[1:]:
                    for _ in range(2 if a == MASK_AT[1] else 1):
                        newton(link_a, b, rs_y[:, 0:T], rs_a[:, 0:T], rs_v[:, 0:T])
                if a == MASK_AT[2]:
                    for t in range(T):
                        ins = dve.tensor_scalar(maskv[:, t, :], xin[:, t, :], mv[:, t, 0:1], rs_y[:, t:t + 1], ALU.subtract, ALU.mult)
                    link_a(b, ins)
                    link_a(b, dve.tensor_scalar(maskv[:, :, :], maskv[:, :, :], 1.0, -1e10, ALU.subtract, ALU.mult))
                for l in range(2):
                    if a == TERMS_AT[l]:
                        dve.wait_ge(t_full, t_value(b, l, 0))
                        ps = tb[:, 0:T * 2 * H].rearrange("p (t c) -> p t c", t=T)
                        link_a(b, dve.tensor_copy(parts[:, :, 0, :], ps))
                        dve.tensor_tensor(sn_res[:, :, :], ps, parts[:, :, 0, :], ALU.subtract).then_inc(t_free, 1)
                        dve.wait_ge(t_free, t_value(b, l, 0) + 1)
                        link_a(b, dve.tensor_copy(parts[:, :, 1, :], sn_res[:, :, :]))
                        dve.tensor_tensor(parts[:, :, 2, :], sn_res[:, :, :], parts[:, :, 1, :], ALU.subtract).then_inc(parts_ready, 1)
                    if a == PARTS_AT[l]:
                        dve.wait_ge(t_full, t_value(b, l, 1))
                        dve.tensor_copy(partsT[:, :], tb[0:KZ, 0:N // 2].bitcast(BF16)).then_inc(t_free, 1)
                        dve.wait_ge(t_free, t_value(b, l, 1) + 1)
                        dve.tensor_scalar(pair_l[:, :], partsT[:, :], cst[0:KZ, C_SELF:C_SELF + 1], cst[0:KZ, C_NEIGH:C_NEIGH + 1],
                                          ALU.mult, ALU.add).then_inc(pair_l_ready, 1)
                    if l == 0 and a == PAIRS_AT[0] + 1:
                        dve.wait_ge(z_full, z_value(b, 0, 0))
                        dve.sem_inc(c_used, 1)
                    for k in units(l, a):
                        dve.wait_ge(z_free, z_value(b, l, k + 1) + 1)
                        if k >= 2:
                            dve.wait_ge(score_ready, unit(b, l, k) - 1)
                        dve.scalar_tensor_tensor(lr[:, k % 2, :], zs[:, k % 2, :], 0.2, zs[:, k % 2, :], ALU.mult, ALU.min)\
                           .then_inc(lrelu_done, 1)
                    for k in units(l, a - SCORE_LAG):
                        t, hp = divmod(k, H // 2)
                        dve.wait_ge(lrelu_done, unit(b, l, k) + 3)
                        if k >= 3:
                            dve.wait_ge(t_full, t_value(b, l, k - 1))
                        dve.nop(nofuse=True)
                        for h in range(2):
                            ins = dve.tensor_tensor_reduce(tt[:, k % 3, h, :], lr[:, k % 2, h * N:(h + 1) * N], maskv[:, t, :], 1.0, 3e38,
                                                           ALU.add, ALU.min, gmn[:, k % 3, h:h + 1])
                        ins.then_inc(score_ready, 1)
                    for t in range(T):
                        if a == done(l, t):
                            dve.wait_ge(pv_done, unit(b, l, 4 * t + 4))
                            o_ = ob[:, 0:H * FE].rearrange("p (h o) -> p h o", h=H)
                            link_a(b, dve.reciprocal(gsum[:, :], o_[:, :, FO]))
                            g_ = go[:, t, :].rearrange("p (h o) -> p h o", h=H)
                            dve.tensor_tensor(g_, o_[:, :, 0:FO], gsum[:, :].unsqueeze(2).broadcast_to([P, H, FO]), ALU.mult)\
                               .then_inc(o_free, 1)
                            dve.wait_ge(o_free, b * 2 * T + l * T + t + 2)
                            dve.tensor_tensor(go[:, t, :], go[:, t, :], rows[:, (4 + l) * D:(5 + l) * D], ALU.add)\
                               .then_inc(gout_ready, 1)
                        if a == done(l, t) + ELU_LAG:
                            dve.wait_ge(gexp_ready, b * 2 * T + l * T + t + 1)
                            link_a(b, dve.tensor_scalar(gex[:, t, :], gex[:, t, :], 1.0, -1.0, ALU.min, ALU.add))
                            ins = dve.scalar_tensor_tensor(gex[:, t, :], go[:, t, :], 0.0, gex[:, t, :], ALU.max, ALU.add)
                            if l == 0:
                                ins.then_inc(gres_ready, 1)
                            else:
                                link_a(b, ins)
                                if t == 0 and not isinstance(b, int):
                                    dve.wait_ge(osum_ready, b * T)
                                link_a(b, dve.tensor_tensor(x1[:, t, :], xin[:, t, :], gex[:, t, :], ALU.add))
                                if t == T - 1:
                                    dve.sem_inc(x_used, 1)
                                link_a(b, dve.bn_stats(stats[:, t, :], x1[:, t, :]))
                if a == OUT_AT:
                    dve.wait_ge(t_full, t_value(b, 0, NU + 2))
                    dve.tensor_copy(gT[:, :, :].rearrange("p k n -> p (k n)"), tb[:, :]).then_inc(t_free, 1)
                if a == LN2_AT[0]:
                    moments(b)
                    link_a(b, dve.tensor_scalar(rs_v[:, 0:T], mv[:, :, 1], LN_EPS, None, ALU.add))
                    link_a(b, dve.scalar_tensor_tensor(rs_v[:, T:2 * T], rs_v[:, 0:T], RMS_EPS, mv[:, :, 1], ALU.mult, ALU.add))
                    first_guess(link_a, b, rs_y[:, :], rs_a[:, :], rs_v[:, :])
                    dve.sem_inc(ln_seed, 1)
                if a == LN2_AT[2]:
                    dve.wait_ge(ln_ready, b + 1)
                    dve.nop(nofuse=True)
                    for t in range(T):
                        ins = dve.tensor_scalar(hn[:, t, :], x1[:, t, :], mv[:, t, 0:1], rs_y[:, T + t:T + t + 1], ALU.subtract, ALU.mult)
                    ins.then_inc(hn_ready, 1)
                if a == HN_AT:
                    dve.wait_ge(t_full, t_value(b, 1, NU + 2))
                    for k in range(KT):
                        ins = dve.tensor_scalar(hT[:, k, :], tb[:, k * N:(k + 1) * N], cols[:, k:k + 1], None, ALU.mult)
                    ins.then_inc(t_free, 1)

            def part(b, w):
                kind, n = w
                ps = bank_of(w)
                if kind == "qkv" and n not in (2, 3):
                    u = n if n < 2 else n - 2
                    which, t = (1, u) if u < 2 else (0, u % 2)
                    dve.wait_ge(raw_ready, b * QU + u + 1)
                    if u >= 4:
                        filled(dve, b, ("turn", u - 4))
                    c_ = rope_c[:, which, t, :].unsqueeze(1).broadcast_to([P, G, HD])
                    ins = dve.tensor_tensor(m1[:, u % 4, :].rearrange("p (h d) -> p h d", h=G),
                                            raw[:, u % 3, :].rearrange("p (h d) -> p h d", h=G), c_, ALU.mult)
                    emptied(dve, b, w)
                    ins = dve.tensor_reduce(ssq[:, u * G:(u + 1) * G], sq[:, u % 3, :].rearrange("p (h d) -> p h d", h=G), AX.X, ALU.add)
                    ins.then_inc(m1_ready, 1)
                    if u in (1, 5, 9):
                        lo, hi = ((0, 2 * G), (2 * G, 6 * G), (6 * G, 10 * G))[(u - 1) // 4]
                        v, y, a = ssq[:, lo:hi], rms[:, lo:hi], rms_a[:, lo:hi]
                        dve.wait_ge(m1_ready, b * QU + u + 4)
                        link_b(b, dve.tensor_scalar(v, v, 1.0 / HD, RMS_EPS, ALU.mult, ALU.add))
                        link_b(b, dve.tensor_scalar(a.bitcast(I32), v.bitcast(I32), 1, None, ALU.logical_shift_right))
                        dve.tensor_scalar(y.bitcast(I32), a.bitcast(I32), -1, MAGIC, ALU.mult, ALU.add).then_inc(seed_ready, 1)
                elif kind == "qkv" and n == 3:
                    dve.wait_ge(m2_ready, b * QU + 5)
                    dve.wait_ge(m1_ready, b * QU + 5)
                    for u in range(T):
                        ins = dve.tensor_tensor(m1[:, u, :], m1[:, u, :], m2[:, u, :], ALU.add)
                    link_b(b, ins)
                    dve.wait_ge(rms_ready, b * 3 + 1)
                    for u in range(T):
                        r_ = m1[:, u, :].rearrange("p (h d) -> p h d", h=G)
                        dve.tensor_tensor(r_, r_, rms[:, u * G:(u + 1) * G].unsqueeze(2).broadcast_to([P, G, HD]), ALU.mult)\
                           .then_inc(k_ready, 1)
                elif kind == "score":
                    g, j = divmod(n, 3)
                    t = min(j, 1)
                    nh, nk = (G, P) if j == 0 else (2, N)
                    h0 = 0 if j == 0 else 2 * (j - 1)
                    if n in (0, 6):
                        dve.wait_ge(rms_ready, b * 3 + 2 + n // 6)
                    filled(dve, b, w)
                    link_b(b, dve.tensor_reduce(smx[:, n, 0:nh], ps[:, :].rearrange("p (h k) -> p h k", h=nh), AX.X, ALU.max))
                    dve.scalar_tensor_tensor(sneg[:, n, 0:nh], smx[:, n, 0:nh], -1.0, rq(g, t, h0, nh), ALU.mult, ALU.mult)\
                       .then_inc(sneg_ready, 1)
                elif kind == "probT":
                    g, j = divmod(n, 3)
                    filled(dve, b, w)
                    if j == 0:
                        if g:
                            filled(dve, b, ("av", 2 * (g - 1)))
                        dve.tensor_copy(pT0[:, :, :].rearrange("p h q -> p (h q)"), ps[:, :]).then_inc(free_of(w), 1)
                    else:
                        if g:
                            filled(dve, b, ("av", 2 * (g - 1) + 1))
                        dve.tensor_copy(pT1[:, :, 2 * (j - 1):2 * j, :], ps[:, :].rearrange("p (m h q) -> p m h q", m=T, h=2))\
                           .then_inc(free_of(w), 1)
                elif kind == "oproj":
                    filled(dve, b, w)
                    if n == 0:
                        dve.wait_ge(hid_ready, b + 1)
                        dve.nop(nofuse=True)
                    dve.tensor_tensor(hid2[:, n, :], ps[:, 0:D], hid[:, n, :], ALU.add).then_inc(free_of(w), 1)
                    emptied(dve, b, w)
                    dve.tensor_tensor_reduce(h2n[:, n, :], hid2[:, n, :], hid2[:, n, :], 1.0, 0.0, ALU.mult, ALU.add, ss2[:, n:n + 1])\
                       .then_inc(hid2_ready, 1)
                    dve.wait_ge(hid2_ready, b * T + n + 1)
                    one = slice(n, n + 1)
                    dve.tensor_scalar(h2_m[:, one], ss2[:, one], -0.5 / D, -0.5 * RMS_EPS, ALU.mult, ALU.add)
                    link_b(b, dve.tensor_scalar(h2_v[:, one], ss2[:, one], 1.0 / D, RMS_EPS, ALU.mult, ALU.add))
                elif kind == "h2T":
                    filled(dve, b, w)
                    for k in range(KT):
                        ins = dve.tensor_scalar(tokT[:, k, n * P:(n + 1) * P], ps[:, k * P:(k + 1) * P], cols[:, KT + k:KT + k + 1], None,
                                                ALU.mult)
                    ins.then_inc(free_of(w), 1)
                elif kind == "gate":
                    filled(dve, b, w)
                    link_b(b, dve.tensor_copy(lg[:, :, :].rearrange("p t e -> p (t e)"), ps[:, 0:T * E]))
                    ins = dve.tensor_reduce(lmx[:, :], lg[:, :, :], AX.X, ALU.max)
                    ins.then_inc(free_of(w), 1)
                    emptied(dve, b, w)
                    for t in range(T):
                        dve.tensor_scalar(lmx[:, t:t + 1], lmx[:, t:t + 1], -1.0, None, ALU.mult).then_inc(lneg_ready, 1)
                elif kind == "updown":
                    dve.wait_ge(tanh_ready, b * JT + n + 1)
                    at = mark_b(dve.scalar_tensor_tensor(ga[:, :], th[:, n % 3, :], 1.0, ps[:, 0:N], ALU.add, ALU.mult))
                    for i in range(*MIXING[n][0:2]):
                        mixing(b, i)
                    dve.wait_ge(dve_b, b * N_B + at)
                    dve.scalar_tensor_tensor(ah[:, n, :], ga[:, :], 0.5, ps[:, N:2 * N], ALU.mult, ALU.mult).then_inc(free_of(w), 1)
                    for i in range(*MIXING[n][1:3]):
                        mixing(b, i)
                    emptied(dve, b, w)
                elif kind == "mixT":
                    filled(dve, b, w)
                    dve.tensor_copy(mixT[:, n * P:(n + 1) * P], ps[0:NP * E, 0:P // 2].bitcast(BF16)).then_inc(free_of(w), 1)
                elif kind == "mix":
                    filled(dve, b, w)
                    j0, j1 = 2 * n, min(2 * n + 2, JT)
                    a_ = ah[:, j0:j1, :].rearrange("p j n -> p (j n)")
                    dve.tensor_tensor(a_, a_, ps[:, 0:(j1 - j0) * N], ALU.mult).then_inc(free_of(w), 1)
                elif kind == "down":
                    filled(dve, b, w)
                    dve.wait_ge(osum_ready, b * T + n + 1)
                    dve.wait_ge(out_free, (b + 1) * 16 * T)
                    dve.tensor_tensor(yo[:, n, :], osum[:, n, :], ps[:, 0:D], ALU.add).then_inc(free_of(w), 1)
                    emptied(dve, b, w)
                    dve.sem_inc(y_ready, 1)

            def reciprocals(b, s):
                for n in summed(s):
                    nh = G if n % 3 == 0 else 2
                    emptied(dve, b, ("score", n))
                    dve.reciprocal(srcp[:, n, 0:nh], ssum[:, n, 0:nh]).then_inc(srcp_ready, 1)

            def second_norm(b, s):
                for t in range(T):
                    one = slice(t, t + 1)
                    y, a, m = h2_y[:, one], h2_a[:, one], h2_m[:, one]
                    if s == NORM2_AT[t][0]:
                        first_guess(link_b, b, y, a, h2_v[:, one])
                    if s in NORM2_AT[t]:
                        for _ in range(1 if s == NORM2_AT[t][0] else 2):
                            link_b(b, dve.scalar_tensor_tensor(a, y, m, y, ALU.mult, ALU.mult))
                            link_b(b, dve.scalar_tensor_tensor(y, a, 1.5, y, ALU.add, ALU.mult))
                    if s == NORM2_AT[t][1]:
                        dve.tensor_scalar(h2n[:, t, :], hid2[:, t, :], h2_y[:, one], None, ALU.mult).then_inc(h2n_ready, 1)

            def mixing(b, i):
                wide = [P, T, E, E]
                mine, other = lex[:, :, :].unsqueeze(3).broadcast_to(wide), lex[:, :, :].unsqueeze(2).broadcast_to(wide)
                tri = cst[:, C_TRI:C_TRI + E * E].rearrange("p (e j) -> p e j", e=E).unsqueeze(1).broadcast_to(wide)
                sums = lmx[:, :].unsqueeze(2).broadcast_to([P, T, E])
                if i == 0:
                    dve.wait_ge(lexp_ready, (b + 1) * T)
                else:
                    dve.wait_ge(dve_b, b * N_B + mixed[0])
                dve.nop(nofuse=True)
                if i in (0, 8):
                    ins = dve.tensor_reduce(lmx[:, :], lex[:, :, :], AX.X, ALU.add)
                elif i in (1, 10):
                    ins = dve.reciprocal(lmx[:, :], lmx[:, :])
                elif i in (2, 11):
                    ins = dve.tensor_tensor(lex[:, :, :], lex[:, :, :], sums, ALU.mult)
                elif i == 3:
                    dve.tensor_tensor(cmp1, other, mine, ALU.is_gt)
                    ins = dve.tensor_tensor(cmp2, other, mine, ALU.is_ge)
                elif i == 4:
                    ins = dve.tensor_tensor(cmp2, cmp2, tri, ALU.mult)
                elif i == 5:
                    ins = dve.tensor_tensor(cmp1, cmp1, cmp2, ALU.max)
                elif i == 6:
                    ins = dve.tensor_reduce(rank[:, :, :], cmp1, AX.X, ALU.add)
                elif i == 7:
                    ins = dve.scalar_tensor_tensor(lex[:, :, :], rank[:, :, :], 2.0, lex[:, :, :], ALU.is_lt, ALU.mult)
                elif i == 9:
                    ins = dve.tensor_scalar(lmx[:, :], lmx[:, :], 1e-9, None, ALU.add)
                elif i == 12:
                    ins = dve.tensor_copy(mixp[:, :, 0, :], lex[:, :, :])
                elif i == 13:
                    ins = dve.tensor_tensor(rank[:, :, :], lex[:, :, :], mixp[:, :, 0, :], ALU.subtract)
                elif i == 14:
                    ins = dve.tensor_copy(mixp[:, :, 1, :], rank[:, :, :])
                elif i == 15:
                    dve.tensor_tensor(mixp[:, :, 2, :], rank[:, :, :], mixp[:, :, 1, :], ALU.subtract).then_inc(mix_ready, 1)
                    return
                mixed[0] = mark_b(ins)

            n_setup = [0]

            def link(ins):
                n_setup[0] += 1
                ins.then_inc(setup_v, 1)
                dve.wait_ge(setup_v, n_setup[0])

            def apply_terms(l):
                for k in range(1 if l == 0 else KT):
                    wx = w0x[:, :] if l == 0 else w1x[:, k, :]
                    np_ = F_IN if l == 0 else P
                    for v in range(2):
                        link(dve.tensor_tensor(wprod[0:np_, :], wx[:, 0:D], rows[0:np_, (2 * l + v) * D:(2 * l + v + 1) * D], ALU.mult))
                        link(dve.tensor_reduce(wx[:, D + v * H:D + (v + 1) * H], wprod[0:np_, :].rearrange("p (h o) -> p h o", h=H),
                                               AX.X, ALU.add))

            def rope_tables():
                for m in range(2):
                    for t in range(T):
                        w_ = qkw[:, m * HD:(m + 1) * HD]
                        link(dve.tensor_tensor(rope_c[:, m, t, :], cst[:, C_COS + t * HD:C_COS + (t + 1) * HD], w_, ALU.mult))
                        for c in range(2):
                            half = slice(c * HD // 2, (c + 1) * HD // 2)
                            sines = cst[:, C_SIN + t * HD + c * HD // 2:C_SIN + t * HD + (c + 1) * HD // 2]
                            other = qkw[:, m * HD + (1 - c) * HD // 2:m * HD + (2 - c) * HD // 2]
                            link(dve.tensor_tensor(rope_s[:, m, t, half], sines, other, ALU.mult))

            dve.wait_ge(in_w0, 32)
            apply_terms(0)
            dve.wait_ge(in_cst, 16)
            link(dve.tensor_copy(identb[:, :], ident))
            for t in range(T):
                link(dve.memset(feat[:, t, :, FO:FE], 1.0))
            dve.sem_inc(z_free, 1)
            dve.sem_inc(t_free, 1)
            dve.sem_inc(o_free, 1)
            dve.sem_inc(lrelu_done, 2)
            dve.sem_inc(m1_ready, 3)
            dve.sem_inc(m2_ready, 3)
            dve.sem_inc(out_free, 16 * T)
            for k in range(BANKS):
                dve.sem_inc(free[k], 1)
            dve.sem_inc(setup_done, 1)
            for s in range(STEPS):
                gat(0, s)
                if s == PARTS_AT[0]:
                    dve.wait_ge(in_gat, 80)
                    apply_terms(1)
                    dve.sem_inc(setup_done, 1)
                if s == PARTS_AT[1]:
                    rope_tables()
                    link(dve.tensor_copy(causal[:, :], cst[:, C_CAUSAL:C_CAUSAL + P]))
                    link(dve.tensor_copy(expert_rows[:, :], spread_in))
                    dve.sem_inc(setup_done, 1)
            assert count[0] == N_A, count
            with dve.Fori(0, B - 1) as b:
                count[:] = [0, 0]
                for s in range(STEPS):
                    gat(b + 1, s)
                    for w in use(s):
                        part(b, w)
                    second_norm(b, s)
                    reciprocals(b, s)
            assert count[1] == N_B, count
            count[:] = [0, 0]
            for s in range(STEPS):
                for w in use(s):
                    part(B - 1, w)
                second_norm(B - 1, s)
                reciprocals(B - 1, s)


def kernel(**inputs):
    import numpy as _np
    import concourse.bacc as _bacc
    from concourse import mybir as _mybir
    from concourse.bass_utils import run_bass_kernel_spmd as _run

    i = {k: _np.asarray(v) for k, v in inputs.items()}
    g = {k[len("L0_xattn_"):]: v for k, v in i.items() if k.startswith("L0_xattn_")}
    f = {k[len("L0_ffn_"):]: v for k, v in i.items() if k.startswith("L0_ffn_")}

    def on_rows(*vectors):
        return _np.concatenate([_np.broadcast_to(v.reshape(1, -1), (P, v.size)) for v in vectors], 1)

    arrays = {
        "x": i["x"],
        "ctxT": i["ctx_512"].transpose(0, 2, 1),
        "w0": g["W0"].transpose(1, 0, 2).reshape(F_IN, D),
        "w1": g["W1"].transpose(1, 0, 2).reshape(D, D),
        "gat_rows": on_rows(g["a_self0"], g["a_neigh0"], g["a_self1"], g["a_neigh1"], g["b0"], g["b1"]),
        "norm_cols": _np.concatenate([f["attn_norm_w"].reshape(KT, P).T, f["ffn_norm_w"].reshape(KT, P).T], 1),
        "qk_rows": on_rows(f["q_norm_w"], f["k_norm_w"]),
        "wqkv": _np.concatenate([f["q_w"], f["k_w"], f["v_w"]], 0).T,
        "wo": f["o_w"].T,
        "wgate": f["gate_w"].T,
        "wgu": _np.stack([f["wg"].reshape(EI, D).T, f["wu"].reshape(EI, D).T]),
        "wd": f["wd"].transpose(0, 2, 1).reshape(EI, D),
        "consts": constants()[0],
        "spread": constants()[1],
    }
    arrays = {k + "_dram": _np.ascontiguousarray(v) for k, v in arrays.items()}
    nc = _bacc.Bacc("TRN2", target_bir_lowering=False, num_devices=1)
    args = [nc.dram_tensor(k, v.shape, _mybir.dt.from_np(v.dtype), kind="ExternalInput").ap() for k, v in arrays.items()]
    args.append(nc.dram_tensor("out_dram", (B, N, D), _mybir.dt.float32, kind="ExternalOutput").ap())
    block_program(nc, *args)
    r = _run(nc, [arrays], core_ids=[0])
    return r.results[0]["out_dram"]
```
